# Optimizing a Trainium2 kernel written in Bass

```python
import numpy as np
import jax
import jax.numpy as jnp

def _softmax(x, axis=-1):
    return jax.nn.softmax(x, axis=axis)

def _gelu(x):
    return jax.nn.gelu(x, approximate=True)

def _silu(x):
    return jax.nn.silu(x)

def _sigmoid(x):
    return jax.nn.sigmoid(x)

def _layernorm(x, axis=-1, eps=1e-05):
    m = jnp.mean(x, axis=axis, keepdims=True)
    v = jnp.var(x, axis=axis, keepdims=True)
    return (x - m) / jnp.sqrt(v + eps)

def _scatter_add(tgt, idx, src, axis=0):
    return tgt.at[idx].add(src)

def _segment_sum(src, seg, n):
    return jax.ops.segment_sum(src, seg, n)
kernel_name = 'mk_gps_d1_gnn_r32_6d92fe'

def setup_inputs(seed: int=0):
    np.random.seed(seed)
    _w = jnp.asarray

    def _rec_inputs():
        import jax
        import jax.numpy as jnp
        _gk = jax.random.key(seed)
        x = -0.0003019 + 1 * jax.random.normal(jax.random.fold_in(_gk, 1), (625, 1024), jnp.float32)
        src = jax.random.randint(jax.random.fold_in(_gk, 2), (10000,), 0, 625, jnp.int32)
        dst = jax.random.randint(jax.random.fold_in(_gk, 3), (10000,), 0, 625, jnp.int32)
        _o = jnp.argsort(dst, stable=True)
        src = src[_o]
        dst = dst[_o]
        return (x, src, dst)
    x, src, dst = _rec_inputs()

    def _L0_gnn_setup():
        import jax, jax.numpy as jnp
        import numpy as np
        N, IN_FEAT, OUT_FEAT, HEADS, E = (625, 1024, 256, 4, 10000)
        NEG_SLOPE = 0.2
        key = jax.random.key(seed)
        k1, k2, k3, k4, k5, k6 = jax.random.split(key, 6)
        h = jax.random.normal(k1, (N, IN_FEAT), dtype=jnp.float32)
        src = jax.random.randint(k2, (E,), 0, N, dtype=jnp.int32)
        dst = jax.random.randint(k3, (E,), 0, N, dtype=jnp.int32)
        W = jax.random.normal(k4, (HEADS, IN_FEAT, OUT_FEAT), dtype=jnp.float32) * (1.0 / np.sqrt(IN_FEAT))
        a_l = jax.random.normal(k5, (HEADS, OUT_FEAT), dtype=jnp.float32) * (1.0 / np.sqrt(OUT_FEAT))
        a_r = jax.random.normal(k6, (HEADS, OUT_FEAT), dtype=jnp.float32) * (1.0 / np.sqrt(OUT_FEAT))
        return {'h': h, 'W': W, 'a_l': a_l, 'a_r': a_r, 'src': src, 'dst': dst}
    _L0_gnn_all = _L0_gnn_setup()
    _L0_gnn_in = {k: v for k, v in _L0_gnn_all.items() if k in ('W', 'a_l', 'a_r')}
    del _L0_gnn_all

    def _L0_mix_setup():
        import jax, jax.numpy as jnp
        import numpy as np
        B, S, D_MODEL, N_HEADS = (4, 256, 1024, 16)
        D_K = D_MODEL // N_HEADS
        key = jax.random.key(seed)
        k1, k2, k3 = jax.random.split(key, 3)
        x = jax.random.normal(k1, (B, S, D_MODEL), dtype=jnp.float32)
        w_qkv = jax.random.normal(k2, (D_MODEL, 3 * D_MODEL), dtype=jnp.float32) * (1.0 / np.sqrt(D_MODEL))
        w_o = jax.random.normal(k3, (D_MODEL, D_MODEL), dtype=jnp.float32) * (1.0 / np.sqrt(D_MODEL))
        return {'x': x, 'w_qkv': w_qkv, 'w_o': w_o}
    _L0_mix_all = _L0_mix_setup()
    _L0_mix_in = {k: v for k, v in _L0_mix_all.items() if k in ('w_qkv', 'w_o')}
    del _L0_mix_all

    def _L0_ffn_setup():
        import jax, jax.numpy as jnp
        import numpy as np
        IN_FEATURES = 1024
        OUT_FEATURES = 1024
        B, S = (8, 128)
        key = jax.random.key(seed)
        kx, kw = jax.random.split(key)
        x = jax.random.normal(kx, (B, S, IN_FEATURES), dtype=jnp.float32)
        weight = jax.random.normal(kw, (OUT_FEATURES, IN_FEATURES), dtype=jnp.float32) * 0.1
        bias = jnp.zeros((OUT_FEATURES,), dtype=jnp.float32)
        return {'x': x, 'weight': weight, 'bias': bias}
    _L0_ffn_all = _L0_ffn_setup()
    _L0_ffn_in = {k: v for k, v in _L0_ffn_all.items() if k in ('weight', 'bias')}
    del _L0_ffn_all
    return {'x': x, 'src': src, 'dst': dst, 'L0_gnn_W': _L0_gnn_in['W'], 'L0_gnn_a_l': _L0_gnn_in['a_l'], 'L0_gnn_a_r': _L0_gnn_in['a_r'], 'L0_mix_w_qkv': _L0_mix_in['w_qkv'], 'L0_mix_w_o': _L0_mix_in['w_o'], 'L0_ffn_weight': _L0_ffn_in['weight'], 'L0_ffn_bias': _L0_ffn_in['bias']}

def reference(x, src, dst, L0_gnn_W, L0_gnn_a_l, L0_gnn_a_r, L0_mix_w_qkv, L0_mix_w_o, L0_ffn_weight, L0_ffn_bias):
    import jax
    import jax.numpy as jnp

    def _L0_gnn_ref(h, W, a_l, a_r, src, dst):
        import jax, jax.numpy as jnp
        import numpy as np
        N, IN_FEAT, OUT_FEAT, HEADS, E = (625, 1024, 256, 4, 10000)
        NEG_SLOPE = 0.2
        z = jnp.einsum('ni,hif->nhf', h, W)
        el = jnp.einsum('nhf,hf->nh', z, a_l)
        er = jnp.einsum('nhf,hf->nh', z, a_r)
        e = jax.nn.leaky_relu(el[src] + er[dst], NEG_SLOPE)
        m = jax.ops.segment_max(e, dst, num_segments=N)
        ex = jnp.exp(e - m[dst])
        s = jax.ops.segment_sum(ex, dst, num_segments=N)
        alpha = ex / s[dst]
        out = jax.ops.segment_sum(alpha[:, :, None] * z[src], dst, num_segments=N)
        return out.reshape(N, HEADS * OUT_FEAT)

    def _L0_mix_ref(x, w_qkv, w_o):
        import jax, jax.numpy as jnp
        import numpy as np
        B, S, D_MODEL, N_HEADS = (4, 256, 1024, 16)
        D_K = D_MODEL // N_HEADS
        b, s, dm = x.shape
        h, d = (N_HEADS, D_K)
        qkv = (x @ w_qkv).reshape(b, s, 3, h, d)
        q, k, v = (qkv[:, :, 0], qkv[:, :, 1], qkv[:, :, 2])
        q = jax.nn.elu(q) + 1.0
        k = jax.nn.elu(k) + 1.0
        kv = jnp.einsum('bnhd,bnhf->bhdf', k, v)
        k_sum = k.sum(axis=1)
        numerator = jnp.einsum('bnhd,bhdf->bnhf', q, kv)
        denominator = jnp.einsum('bnhd,bhd->bnh', q, k_sum)[..., None] + 1e-06
        attn = (numerator / denominator).reshape(b, s, dm)
        return attn @ w_o

    def _L0_ffn_ref(x, weight, bias):
        import jax, jax.numpy as jnp
        import numpy as np
        IN_FEATURES = 1024
        OUT_FEATURES = 1024
        B, S = (8, 128)
        w_scale = jnp.mean(jnp.abs(weight))
        q_weight = jnp.sign(weight) * (jnp.abs(weight) > 0.5 * w_scale).astype(weight.dtype)
        i_scale = jnp.max(jnp.abs(x)) / 127.0
        q_input = jnp.clip(jnp.round(x / i_scale), -128.0, 127.0)
        out = jnp.einsum('bsk,ok->bso', q_input, q_weight) * w_scale * i_scale
        out = out + bias
        return out
    xn = _layernorm(x, axis=-1)
    x = x + _L0_gnn_ref(xn, L0_gnn_W, L0_gnn_a_l, L0_gnn_a_r, src, dst) + _L0_mix_ref(xn[None], L0_mix_w_qkv, L0_mix_w_o)[0]
    x = x + _L0_ffn_ref(_layernorm(x, axis=-1)[None], L0_ffn_weight, L0_ffn_bias)[0]
    return x

_drawn_inputs = setup_inputs


def setup_inputs(seed=0):
    import zlib

    import numpy as np

    out = dict(_drawn_inputs(seed))
    spreads = {'L0_ffn_bias': (0.0, 0.1)}
    factors = {}
    for name, (base, spread) in spreads.items():
        noise = np.random.default_rng([zlib.crc32(name.encode()), seed]).standard_normal(out[name].shape)
        drawn = base * np.exp(spread * noise) if base else spread * noise
        out[name] = jnp.asarray(drawn.astype(out[name].dtype))
    for name, factor in factors.items():
        out[name] = (out[name] * factor).astype(out[name].dtype)
    return out
```

```python
import concourse.bass as bass
from concourse import mybir
from contextlib import ExitStack


def gps_layer(nc, x, edges, a_lr, weights, ffn_weights, bias, out):
    f32, f32r, bf16 = mybir.dt.float32, mybir.dt.float32r, mybir.dt.bfloat16
    f16, i16, i32, fp8 = mybir.dt.float16, mybir.dt.int16, mybir.dt.int32, mybir.dt.float8e4
    ALU, ACT = mybir.AluOpType, mybir.ActivationFunctionType
    AX = mybir.AxisListType
    ds = bass.ds

    N, D = x.shape
    P = 125
    NT = N // P
    KT = D // 128
    HEADS, F = 4, 256
    CH = 512
    DK, PAIR = 64, 128
    NPAIR = D // PAIR
    HP = NPAIR // 2
    E = edges.shape[1]
    ET = E // P
    SEG = ET // NT
    RING = SEG // 2
    STATS_AT = [0, 1, 2, 3, 5, 6, 6, 7, 7]
    QUAD = 4
    HALF = (N + 1) // 2 + 1
    NPAD = 2 * ((N + 1) // 2)
    BASE = 4096
    GROUP_SEGS = [(0, 1), (2, 3), (4,)]
    NG = len(GROUP_SEGS)
    assert max(len(g) for g in GROUP_SEGS) * SEG * P < BASE and NT * P == N and ET * P == E
    MAGIC = 12582912.0
    NEG = -1.0e38
    NEG_FLOOR = -4.0e37
    SLOPE, LN_EPS, DEN_EPS = 0.2, 1e-5, 1e-6
    Z_CH, KV_CH = 2, 4
    N1 = N // 2 // 2 * 2
    HALVES = [(slice(0, N1), slice(0, N1)), (slice(N1 - N % 2, N), slice(N1, N))]
    RQ = (Z_CH + KV_CH) * KT
    UPS = 2 * NT
    NU = D // CH * KT

    ctx = ExitStack()
    with ctx:
        base = (nc.sbuf_base + 31) // 32 * 32
        AREA = 60480
        RAW, WHI, WLO = 126016, 134208, 142400
        KVO, CNT, MSK, ELB, GAT = 150592, 154752, 161024, 167296, 172320
        PHI, TERN, TMP, FRAW, IOTA, END = 174752, 184992, 193184, 203424, 207520, 208800
        ctx.enter_context(nc.sbuf_tensor("arena", [128, END], mybir.dt.uint8))

        def at(name, shape, dtype, offset):
            return nc.alloc_sbuf_tensor_at(name, shape, dtype, offset=base + offset)

        def sb(name, shape, dtype=f32):
            return ctx.enter_context(nc.sbuf_tensor(name, shape, dtype))

        x_sb = at("x_sb", [P, NT, D], f32, 0)
        act_hi = at("act_hi", [128, KT, N], f32r, 20480)
        act_lo = at("act_lo", [128, KT, N], f32r, 40480)
        z_hi = at("z_hi", [P, NT, D], f32r, AREA)
        z_lo = at("z_lo", [P, NT, D], f32r, AREA + 20480)
        k_sb = at("k_sb", [P, NT, CH], f32, AREA + 40960)
        v_sb = at("v_sb", [P, NT, HP, PAIR + 1], f32, AREA + 51200)
        onehot_dst = at("onehot_dst", [P, RING, NPAD], bf16, AREA)
        onehot_src = at("onehot_src", [P, RING, HALF], bf16, AREA + 20032)
        csum = at("csum", [P, NT, HALF], f32, AREA + 32768)
        row_t_sb = at("row_t_sb", [128, 2, 4, P], f32, AREA + 40960)
        alr = at("alr", [P, 2, D], f32, AREA + 48512)
        edge_i = at("edge_i", [P, 2, ET], i32, AREA + 56704)
        half_i = at("half_i", [P, 2, ET], i32, AREA + 57344)
        dst_f = at("dst_f", [P, ET], f32, AREA + 57984)
        src_half = at("src_half", [P, ET], f32, AREA + 58304)
        src_worth = at("src_worth", [P, ET], f32, AREA + 58624)
        wo_hi = at("wo_hi", [128, KT, D], f32r, AREA)
        wo_lo = at("wo_lo", [128, KT, D], f32r, AREA + 32768)
        w_raw = at("w_raw", [128, QUAD, CH], f32, RAW)
        w_hi = at("w_hi", [128, QUAD, CH], f32r, WHI)
        w_lo = at("w_lo", [128, QUAD, CH], f32r, WLO)
        tern = at("tern", [128, KT, D], fp8, TERN)
        kv_blocks = at("kv_blocks", [128, NPAIR, PAIR + 2], f32, KVO)
        counts = at("counts", [P, NT, NPAD], i16, CNT)
        no_edge = at("no_edge", [P, NT, NPAD], bf16, MSK)
        el_rows = at("el_rows", [P, 2, N], f32, ELB)
        q_t = at("q_t", [128, NPAIR, N], f32, CNT)
        packed = at("packed", [P, NG, NT, HALF], f32, GAT)
        score = at("score", [P, 2, N], f32, GAT)
        exp_a = at("exp_a", [P, N], f32, GAT + 5024)
        exp_b = at("exp_b", [P, N], f32, GAT + 7552)
        prob = at("prob", [P, 2, N], f32, GAT + 10080)
        pt_hi = at("pt_hi", [P, NT, P], f32r, GAT + 15104)
        pt_lo = at("pt_lo", [P, NT, P], f32r, GAT + 17632)
        diag = at("diag", [P, 2, NT, P], f32, FRAW)
        junk = at("junk", [P, F], f32, GAT)
        centred = at("centred", [P, NT, D], f32, RAW)
        f_raw = at("f_raw", [128, 2, CH], f32, FRAW)
        above = at("above", [128, 2, CH], fp8, IOTA)
        bias_sb = at("bias_sb", [P, D], f32, PHI)
        quant_t = at("quant_t", [128, 2, KT, 128], bf16, PHI + 4096)
        tmp = at("tmp", [P, NT, CH], f32, TMP)
        unpack = at("unpack", [P, NT, HALF], f32, TMP)
        rows = at("rows", [P, 2, D], f32, TMP)

        iota = at("iota", [P, NPAD], f16, IOTA)
        ident = sb("ident", [128, 128])
        ones = sb("ones", [128, 128])
        zeros = sb("zeros", [P, P], f16)
        bn = sb("bn", [P, 2, 6])
        mv = sb("mv", [P, 2])
        ln = sb("ln", [P, NT, 9])
        elr = sb("elr", [P, NT, 2 * HEADS])
        sm = sb("sm", [P, UPS, 6])
        ssum = sb("ssum", [P, UPS])
        rsum = sb("rsum", [P, UPS])
        den = sb("den", [P, 2, 2 * NPAIR])
        amax = sb("amax", [P, NT + 1])
        gmax = sb("gmax", [1, 1])
        abs_sum = sb("abs_sum", [128, NU + 1])
        scales = sb("scales", [128, 8])

        ps = ctx.enter_context(nc.psum_tensor("ps", [128, 8, 512], f32))
        pt_ps = ps[:, 5:8, :].rearrange("p b (c q) -> p (b c) q", q=128)
        AGG = 7

        def sem(name):
            return ctx.enter_context(nc.semaphore(name))

        edges_in, alr_in, bias_in = sem("edges_in"), sem("alr_in"), sem("bias_in")
        row_t_in = sem("row_t_in")
        x_in = [sem(f"x_in{t}") for t in range(NT)]
        raw_in = [sem(f"raw_in{s}") for s in range(QUAD)]
        f_in = [sem(f"f_in{s}") for s in range(2)]
        consts = sem("consts")
        kv_zero = sem("kv_zero")
        idx = sem("idx")
        oh_ready, oh_used = sem("oh_ready"), sem("oh_used")
        count_done = sem("count_done")
        bank_free = sem("bank_free")
        ln_a, ln_std = sem("ln_a"), sem("ln_std")
        row_mid, row_ready, row_t = sem("row_mid"), sem("row_ready"), sem("row_t")
        act_ready = sem("act_ready")
        up = sem("up")
        w_hi_ready, w_ready = sem("w_hi_ready"), sem("w_ready")
        w_used = sem("w_used")
        proj_done = sem("proj_done")
        z_hi_ready, z_used = sem("z_hi_ready"), sem("z_used")
        el = sem("el")
        diag_ready = sem("diag_ready")
        el_ps, el_free = sem("el_ps"), sem("el_free")
        st = sem("st")
        exps = sem("exps")
        pr = sem("pr")
        pt_done, pt_hi_ready, pt_ready = sem("pt_done"), sem("pt_hi_ready"), sem("pt_ready")
        agg_done, agg_free = sem("agg_done"), sem("agg_free")
        rs = sem("rs")
        k_min, k_exp, k_ready = sem("k_min"), sem("k_exp"), sem("k_ready")
        q_done, q_min, q_exp, q_ready = sem("q_done"), sem("q_min"), sem("q_exp"), sem("q_ready")
        ones_v, kv_done, kv_free = sem("ones_v"), sem("kv_done"), sem("kv_free")
        f_abs, fscale, fs_ps = sem("f_abs"), sem("fscale"), sem("fs_ps")
        f_above, f_tern = sem("f_above"), sem("f_tern")
        num_done, at_v, attn_ready = sem("num_done"), sem("at_v"), sem("attn_ready")
        attn_t, attn_hi, attn_lo = sem("attn_t"), sem("attn_hi"), sem("attn_lo")
        wo_done, x1, centred_in = sem("wo_done"), sem("x1"), sem("centred_in")
        gm, gm_ps = sem("gm"), sem("gm_ps")
        quant, quant_ps, quant_ready = sem("quant"), sem("quant_ps"), sem("quant_ready")
        biased, ffn_done, y_ready, stored = sem("biased"), sem("ffn_done"), sem("y_ready"), sem("stored")

        X1S = 14
        LNS = 10
        ELS = 4

        TERN_FIRST = 6
        NUNIT = HEADS * NT
        UNIT_STEPS = [5, 6, 7, 9, 10, 11, 12, 13, 14, 15]
        EL_STEP = 2

        def unit(u):
            return u // NT, u % NT

        def stream_q(i):
            return RQ + i if i < QUAD else RQ + QUAD + 2 * (i - QUAD) + 1

        def stream_o(i):
            return RQ + QUAD + 2 * i if i < NU - QUAD else RQ + NU + i

        NSTREAM = RQ + 2 * NU
        EARLY = RQ + QUAD

        block = ctx.enter_context(nc.Block())

        @block.sync
        def _(sp):
            sp.dma_start(edge_i[:], edges.rearrange("a (p t) -> p a t", p=P)).then_inc(edges_in, 16)
            for t in range(NT):
                sp.dma_start(x_sb[:, t, :], x[t * P:(t + 1) * P, :]).then_inc(x_in[t], 16)
            for s in range(QUAD):
                sp.dma_start(w_raw[:, s, :], weights[s]).then_inc(raw_in[s], 16)
            sp.dma_start(alr[:], bass.AP(a_lr.tensor, 0, [[0, P], [1, 2 * D]])).then_inc(alr_in, 16)

            def load_quad(q):
                for s in range(QUAD):
                    sp.wait_ge(w_ready, q * QUAD + (s + 1 - QUAD))
                    sp.dma_start(w_raw[:, s, :], weights[ds(q * QUAD + s, 1)].rearrange("a p n -> p (a n)"))\
                      .then_inc(raw_in[s], 16)

            for s in range(2):
                sp.dma_start(f_raw[:, s, :], ffn_weights[s]).then_inc(f_in[s], 16)
            with sp.Fori(1, NU // 2) as h:
                for s in range(2):
                    sp.wait_ge(f_abs, h * 2 + (s - 1))
                    sp.dma_start(f_raw[:, s, :], ffn_weights[ds(h * 2 + s, 1)].rearrange("a p n -> p (a n)"))\
                      .then_inc(f_in[s], 16)
            QA = EARLY // QUAD + 1
            with sp.Fori(1, QA) as q:
                load_quad(q)
            for s in range(2):
                sp.wait_ge(el_ps, 2 * 2)
                sp.dma_start(f_raw[:, s, :], ffn_weights[s]).then_inc(f_in[s], 16)
            with sp.Fori(QA, NSTREAM // QUAD) as q:
                load_quad(q)
                for s in range(2):
                    u = (q - QA) * 2 + (s + 2)
                    sp.wait_ge(f_tern, u - 1)
                    sp.dma_start(f_raw[:, s, :], ffn_weights[ds(u, 1)].rearrange("a p n -> p (a n)"))\
                      .then_inc(f_in[s], 16)
            for u in range(2 + 2 * (NSTREAM // QUAD - QA), NU):
                sp.wait_ge(f_tern, u - 1)
                sp.dma_start(f_raw[:, u % 2, :], ffn_weights[u]).then_inc(f_in[u % 2], 16)
            sp.wait_ge(q_done, 1)
            sp.dma_start(bias_sb[:], bass.AP(bias.tensor, 0, [[0, P], [1, D]])).then_inc(bias_in, 16)
            for t in range(NT):
                for c in range(2):
                    sp.wait_ge(y_ready, 2 * t + c + 1)
                    sp.dma_start(out[t * P:(t + 1) * P, c * CH:(c + 1) * CH],
                                 x_sb[:, t, c * CH:(c + 1) * CH]).then_inc(stored, 16)
            sp.wait_ge(stored, 16 * 2 * NT)

        @block.gpsimd
        def _(pool):
            pool.iota(iota[:], [[1, NPAD]], base=0, channel_multiplier=0,
                      allow_small_or_imprecise_dtypes=True).then_inc(consts, 1)
            pool.memset(zeros[:], 0.0).then_inc(consts, 1)
            pool.memset(ones[:], 1.0).then_inc(consts, 1)
            pool.memset(ident[:], 0.0).then_inc(consts, 1)
            pool.wait_ge(consts, 4)
            pool.affine_select(out=ident[:], in_=ident[:], compare_op=ALU.not_equal, fill=1.0, base=0,
                               pattern=[[-1, 128]], channel_multiplier=1).then_inc(consts, 1)
            pool.memset(kv_blocks[:], 0.0).then_inc(kv_zero, 1)

            def lo_quad(q):
                for s in range(QUAD):
                    pool.wait_ge(w_hi_ready, q * QUAD + (s + 1))
                    pool.tensor_tensor(w_lo[:, s, :], w_raw[:, s, :], w_hi[:, s, :].bitcast(f32),
                                       ALU.subtract).then_inc(w_ready, 1)

            lo_quad(0)
            for t in range(NT):
                for b in range(2):
                    pool.wait_ge(row_t_in, 2 * t + b + 1)
                    sl = (slice(None), slice(4 * b, 4 * b + 4), slice(t * P, (t + 1) * P))
                    pool.tensor_tensor(act_lo[sl], row_t_sb[:, b, :, :], act_hi[sl].bitcast(f32),
                                       ALU.subtract).then_inc(act_ready, 1)
            with pool.Fori(1, EARLY // QUAD) as q:
                lo_quad(q)

            def lo_q(i):
                pool.wait_ge(w_hi_ready, stream_q(i) + 1)
                pool.tensor_tensor(w_lo[:, i % QUAD, :], w_raw[:, stream_q(i) % QUAD, :],
                                   w_hi[:, i % QUAD, :].bitcast(f32), ALU.subtract).then_inc(w_ready, 1)

            def lo_o(i):
                c, k = i // KT, i % KT
                pool.wait_ge(w_hi_ready, stream_o(i) + 1)
                pool.tensor_tensor(wo_lo[:, k, c * CH:(c + 1) * CH], w_raw[:, stream_o(i) % QUAD, :],
                                   wo_hi[:, k, c * CH:(c + 1) * CH].bitcast(f32),
                                   ALU.subtract).then_inc(w_ready, 1)

            for i in range(NU):
                lo_o(i)
                if i + QUAD < NU:
                    lo_q(i + QUAD)
            pool.wait_ge(bias_in, 16)
            for t in range(NT):
                pool.wait_ge(centred_in, t + 1)
                pool.tensor_tensor(x_sb[:, t, :], x_sb[:, t, :], bias_sb[:], ALU.add).then_inc(biased, 1)

        @block.scalar
        def _(act):
            def hi_unit(slot):
                act.activation(w_hi[:, slot, :], w_raw[:, slot, :], ACT.Copy).then_inc(w_hi_ready, 1)

            def row(t):
                act.wait_ge(ln_a, LNS * t + 5)
                act.activation(ln[:, t, 1:2], ln[:, t, 0:1], ACT.Sqrt).then_inc(ln_std, 1)
                if t >= 2:
                    act.wait_ge(row_t, 2 * (t - 1))
                act.activation(rows[:, t % 2, :], x_sb[:, t, :], ACT.Identity, bias=ln[:, t, 7:8]).then_inc(row_mid, 1)
                act.wait_ge(row_mid, t + 1)
                act.wait_ge(ln_a, LNS * (t + 1))
                act.activation(rows[:, t % 2, :], rows[:, t % 2, :], ACT.Identity, scale=ln[:, t, 6:7])\
                   .then_inc(row_ready, 1)

            def split_rows(t):
                for b in range(2):
                    src = pt_ps[:, 4 * b:4 * b + 4, :P]
                    act.wait_ge(row_t, 2 * t + b + 1)
                    act.activation(act_hi[:, 4 * b:4 * b + 4, t * P:(t + 1) * P], src, ACT.Copy)
                    if t >= 1:
                        act.wait_ge(act_ready, 2 * (t - 1) + b + 1)
                    act.activation(row_t_sb[:, b, :, :], src, ACT.Copy).then_inc(row_t_in, 1)

            def copy_counts(g):
                for nt in range(NT):
                    act.wait_ge(count_done, g * NT + nt + 1)
                    act.activation(packed[:, g, nt, :], ps[:P, nt, :HALF], ACT.Copy).then_inc(bank_free, 1)

            def abs_of(pair):
                for u in (2 * pair, 2 * pair + 1):
                    act.wait_ge(f_in[u % 2], 16 * (u // 2 + 1))
                    act.activation(f_raw[:, u % 2, :], f_raw[:, u % 2, :], ACT.Abs,
                                   accum_out=abs_sum[:, u:u + 1]).then_inc(f_abs, 1)

            row(0)
            for s in range(QUAD):
                act.wait_ge(raw_in[s], 16)
                hi_unit(s)
            row(1)
            abs_of(0)
            for t in range(NT):
                split_rows(t)
                if t + 2 < NT:
                    abs_of(t * 2 + 1)
                    row(t + 2)
                    abs_of(t * 2 + 2)
                elif t + 2 == NT:
                    abs_of(NU // 2 - 1)
                if t in (0, 2):
                    copy_counts(t // 2)
            copy_counts(2)

            def step_split(ci, k, q):
                s = k % QUAD
                act.wait_ge(raw_in[s], q * 16 + 16)
                if k < KT - 1:
                    act.wait_ge(w_used, ci * (KT - 1) + (k + 1))
                else:
                    act.wait_ge(proj_done, ci * NT + NT)
                hi_unit(s)

            with act.Fori(0, Z_CH) as c:
                for k in range(KT - 1):
                    step_split(c, k, c * 2 + (k // QUAD + 1))
                for nt in range(NT):
                    act.wait_ge(proj_done, c * NT + (nt + 1))
                    act.wait_ge(z_used, c * NT + (nt + 1))
                    act.activation(tmp[:, nt, :], ps[:P, nt, :], ACT.Copy).then_inc(bank_free, 1)
                step_split(c, KT - 1, c * 2 + 2)
                for nt in range(NT):
                    act.wait_ge(bank_free, (c + NG) * NT + (nt + 1))
                    act.activation(z_hi[:, nt, ds(c * CH, CH)], tmp[:, nt, :], ACT.Copy).then_inc(z_hi_ready, 1)

            def phi(dst, ci, round_, between):
                def exp(nt):
                    act.wait_ge(k_min, round_ * NT + (nt + 1))
                    act.activation(dst[:, nt, :], dst[:, nt, :], ACT.Exp).then_inc(k_exp, 1)

                for nt in range(NT):
                    act.wait_ge(proj_done, ci * NT + (nt + 1))
                    act.wait_ge(k_ready, round_ * NT + (nt + 1))
                    act.activation(tmp[:, nt, :], ps[:P, nt, :], ACT.Copy).then_inc(bank_free, 1)
                between()
                for nt in range(NT):
                    exp(nt)

            def exps_of(u, un):
                b = u % 2
                act.wait_ge(st, un * 6 + 6)
                act.wait_ge(pr, un * 2 + 1)
                act.activation(exp_a[:], score[:, b, :], ACT.Exp, bias=sm[:, u, 2:3]).then_inc(exps, 1)
                act.activation(exp_b[:], score[:, b, :], ACT.Exp, bias=sm[:, u, 3:4], scale=SLOPE).then_inc(exps, 1)

            with act.Fori(0, 2) as j:
                for g in range(2 * KT):
                    if g == EL_STEP + 1:
                        act.wait_ge(el_ps, j * 2 + 2)
                        for a in range(2):
                            act.activation(el_rows[:, a, :].rearrange("p (c q) -> p c q", q=P),
                                           pt_ps[:P, a * NT:(a + 1) * NT, :P], ACT.Copy).then_inc(el_free, 1)
                        exps_of(0, j * UPS)
                    if g in UNIT_STEPS:
                        u = UNIT_STEPS.index(g)
                        act.wait_ge(pt_done, j * UPS + (u + 1))
                        act.wait_ge(agg_done, j * UPS + (u + 1))
                        act.activation(pt_hi[:], pt_ps[:P, 0:NT, :P], ACT.Copy).then_inc(pt_hi_ready, 1)
                        if u + 1 < UPS:
                            exps_of(u + 1, j * UPS + (u + 1))
                    def split():
                        ci = j * 2 + (Z_CH + g // KT)
                        step_split(ci, g % KT, ci * 2 + (g % KT // QUAD + 1))

                    if g == KT - 1:
                        phi(k_sb, j * 2 + Z_CH, j, split)
                    elif g == 2 * KT - 1:
                        for nt in range(NT):
                            act.wait_ge(proj_done, (j * 2 + (Z_CH + 1)) * NT + (nt + 1))
                            act.wait_ge(ones_v, 1)
                            act.wait_ge(kv_done, j * 2 + 1)
                            act.activation(v_sb[:, nt, :, 0:PAIR],
                                           ps[:P, nt, :].rearrange("p (r f) -> p r f", f=PAIR),
                                           ACT.Copy).then_inc(bank_free, 1)
                        split()
                    else:
                        split()

            def hi_at(dst, pos):
                act.wait_ge(raw_in[pos % QUAD], 16 * (pos // QUAD + 1))
                act.activation(dst, w_raw[:, pos % QUAD, :], ACT.Copy).then_inc(w_hi_ready, 1)

            def hi_q(i):
                if i + QUAD < NU:
                    if i % 2 == 0:
                        act.wait_ge(w_used, (Z_CH + KV_CH) * (KT - 1) + i // 2 + 1)
                    else:
                        act.wait_ge(q_done, i + 1)
                    hi_at(w_hi[:, i % QUAD, :], stream_q(i + QUAD))

            def exp_q(r):
                for h, (_, kept) in enumerate(HALVES):
                    act.wait_ge(q_min, 2 * r + h + 1)
                    act.activation(q_t[:, r, kept], q_t[:, r, kept], ACT.Exp).then_inc(q_exp, 1)

            act.wait_ge(agg_done, NUNIT + 1)
            act.wait_ge(kv_done, 2 * 2 + 1)
            for i in range(NU):
                hi_at(wo_hi[:, i % KT, i // KT * CH:(i // KT + 1) * CH], stream_o(i))
                hi_q(i)
                if i % 2 == 1:
                    exp_q(i // 2)

            def second_ln(t):
                act.wait_ge(x1, X1S * t + 7)
                act.activation(centred[:, t, :], x_sb[:, t, :], ACT.Identity, bias=ln[:, t, 7:8]).then_inc(centred_in, 1)
                act.activation(ln[:, t, 1:2], ln[:, t, 0:1], ACT.Sqrt).then_inc(ln_std, 1)

            for t in range(NT):
                for b in range(2):
                    act.wait_ge(attn_t, 2 * t + b + 1)
                    act.activation(act_hi[:, 4 * b:4 * b + 4, t * P:(t + 1) * P],
                                   ps[:, 4 + b, :].rearrange("p (c q) -> p c q", q=128)[:, :, :P],
                                   ACT.Copy).then_inc(attn_hi, 1)
                if t >= 1:
                    second_ln(t - 1)
            second_ln(NT - 1)
            for t in range(NT):
                for b in range(2):
                    act.wait_ge(quant_ps, 2 * t + b + 1)
                    if t >= 2:
                        act.wait_ge(ffn_done, 2 * (t - 1))
                    act.activation(quant_t[:, t % 2, 4 * b:4 * b + 4, :P],
                                   ps[:, 6 + b, :].rearrange("p (c q) -> p c q", q=128)[:, :, :P],
                                   ACT.Copy, bias=-MAGIC).then_inc(quant_ready, 1)

        @block.vector
        def _(dve):
            def rstd_step(i, c, signal, n):
                if i > 0:
                    dve.wait_ge(signal, n + i)
                if i == 0:
                    dve.reciprocal(c[:, 2:3], c[:, 1:2]).then_inc(signal, 1)
                elif i == 1:
                    dve.tensor_tensor(c[:, 3:4], c[:, 2:3], c[:, 2:3], ALU.mult).then_inc(signal, 1)
                elif i == 2:
                    dve.tensor_tensor(c[:, 4:5], c[:, 3:4], c[:, 0:1], ALU.mult).then_inc(signal, 1)
                elif i == 3:
                    dve.tensor_scalar(c[:, 5:6], c[:, 4:5], -0.5, 1.5, ALU.mult, ALU.add).then_inc(signal, 1)
                else:
                    dve.tensor_tensor(c[:, 6:7], c[:, 5:6], c[:, 2:3], ALU.mult).then_inc(signal, 1)

            dve.wait_ge(edges_in, 16)
            dve.tensor_copy(dst_f[:], edge_i[:, 1, :]).then_inc(idx, 1)
            dve.tensor_scalar(half_i[:, 0, :], edge_i[:, 0, :], 1, None, ALU.arith_shift_right).then_inc(idx, 1)
            dve.tensor_scalar(half_i[:, 1, :], edge_i[:, 0, :], 1, None, ALU.bitwise_and).then_inc(idx, 1)
            dve.wait_ge(idx, 3)
            dve.tensor_copy(src_half[:], half_i[:, 0, :]).then_inc(idx, 1)
            dve.tensor_scalar(src_worth[:], half_i[:, 1, :], float(BASE - 1), 1.0, ALU.mult, ALU.add).then_inc(idx, 1)
            dve.wait_ge(idx, 5)
            dve.wait_ge(consts, 5)

            def onehots(n, s):
                dve.wait_ge(oh_used, n * SEG + (s + 1))
                dve.tensor_scalar(onehot_dst[:, s % RING, :], iota[:], dst_f[:, ds(n * SEG + s, 1)], None,
                                  ALU.is_equal).then_inc(oh_ready, 1)
                dve.tensor_scalar(onehot_src[:, s % RING, :], iota[:, :HALF], src_half[:, ds(n * SEG + s, 1)],
                                  src_worth[:, ds(n * SEG + s, 1)], ALU.is_equal, ALU.mult).then_inc(oh_ready, 1)

            def statistics(n, step):
                row = x_sb[:, ds(n, 1), :].rearrange("p a d -> p (a d)")
                c = ln[:, ds(n, 1), :].rearrange("p a d -> p (a d)")
                if step < 2:
                    if step == 0:
                        for a in ([n] if isinstance(n, int) else range(2, NT)):
                            dve.wait_ge(x_in[a], 16)
                    dve.bn_stats(bn[:, step, :], row[:, step * CH:(step + 1) * CH]).then_inc(ln_a, 1)
                elif step == 2:
                    dve.bn_aggr(mv[:], bn[:].rearrange("p a b -> p (a b)")).then_inc(ln_a, 1)
                elif step == 3:
                    dve.wait_ge(ln_a, n * LNS + 3)
                    dve.tensor_scalar(c[:, 0:1], mv[:, 1:2], LN_EPS, None, ALU.add).then_inc(ln_a, 1)
                    dve.tensor_scalar(c[:, 7:8], mv[:, 0:1], -1.0, None, ALU.mult).then_inc(ln_a, 1)
                else:
                    if step == 4:
                        dve.wait_ge(ln_std, n + 1)
                    rstd_step(step - 4, c, ln_a, n * LNS + 5)

            def segment(n, rows_at):
                for s in range(SEG):
                    steps = [(t, i) for t, first in rows_at for i, at_ in enumerate(STATS_AT) if first + at_ == s]
                    for t, step in steps:
                        if step == 2:
                            dve.wait_ge(ln_a, t * LNS + 2)
                    onehots(n, s)
                    for t, step in steps:
                        statistics(t, step)

            segment(0, [(0, 0), (1, 8)])
            with dve.Fori(1, NT - 1) as n:
                segment(n, [(n + 1, 2)])
            segment(NT - 1, [])
            dve.wait_ge(f_abs, NU)
            dve.reduce_sum(abs_sum[:, NU:NU + 1], abs_sum[:, :NU], axis=AX.X).then_inc(fscale, 1)
            dve.wait_ge(row_t, 2 * NT)

            ups = 0
            dve.wait_ge(bank_free, NG * NT)
            for g in range(NG):
                pk, un, cs = packed[:, g, :, :], unpack[:], csum[:]
                dve.tensor_scalar(un, pk, -BASE / 2.0 + 48.0, 1.0 / BASE, ALU.add, ALU.mult).then_inc(up, 1)
                ups += 1
                dve.wait_ge(up, ups)
                dve.tensor_scalar(un, un, MAGIC, MAGIC, ALU.add, ALU.subtract).then_inc(up, 1)
                ups += 1
                dve.wait_ge(up, ups)
                dve.scalar_tensor_tensor(pk, un, -float(BASE), pk, ALU.mult, ALU.add).then_inc(up, 1)
                if g == 0:
                    dve.tensor_copy(cs, un).then_inc(up, 1)
                elif g < NG - 1:
                    dve.tensor_tensor(cs, cs, un, ALU.add).then_inc(up, 1)
                else:
                    dve.tensor_tensor(counts[:, :, 1:NPAD:2], cs[:, :, :NPAD // 2], un[:, :, :NPAD // 2],
                                      ALU.add).then_inc(up, 1)
                ups += 2
                dve.wait_ge(up, ups)
            for g in range(1, NG - 1):
                dve.tensor_tensor(packed[:, 0, :, :], packed[:, 0, :, :], packed[:, g, :, :], ALU.add).then_inc(up, 1)
                ups += 1
                dve.wait_ge(up, ups)
            dve.tensor_tensor(counts[:, :, 0:NPAD:2], packed[:, 0, :, :NPAD // 2],
                              packed[:, NG - 1, :, :NPAD // 2], ALU.add).then_inc(up, 1)
            ups += 1
            dve.wait_ge(up, ups)
            dve.tensor_scalar(no_edge[:], counts[:], 0.0, NEG, ALU.is_equal, ALU.mult).then_inc(up, 1)
            ups += 1
            dve.wait_ge(up, ups)
            dve.sem_inc(z_used, NT)

            dve.wait_ge(alr_in, 16)
            dve.sem_inc(el, 1)
            def take_z(c):
                for nt in range(NT):
                    for a in range(2):
                        for side in range(2):
                            if a == 0 and side == 0:
                                dve.wait_ge(bank_free, (c + NG) * NT + (nt + 1))
                            dve.wait_ge(el, (c * NT + nt) * ELS + (2 * a + side + 1))
                            col = side * HEADS + 2 * c + a
                            dve.scalar_tensor_tensor(
                                out=junk[:], in0=tmp[:, nt, a * F:(a + 1) * F], scalar=1.0,
                                in1=alr[:, side, c * CH + a * F:c * CH + (a + 1) * F], op0=ALU.mult, op1=ALU.mult,
                                accum_out=elr[:, nt, col:col + 1]).then_inc(el, 1)
                    dve.wait_ge(el, (c * NT + nt) * ELS + (ELS + 1))
                    dve.wait_ge(z_hi_ready, c * NT + (nt + 1))
                    dve.tensor_tensor(z_lo[:, nt, c * CH:(c + 1) * CH], tmp[:, nt, :],
                                      z_hi[:, nt, c * CH:(c + 1) * CH].bitcast(f32), ALU.subtract).then_inc(z_used, 1)

            def diagonals(j):
                for a in range(2):
                    if j > 0:
                        dve.wait_ge(el_ps, a + 1)
                    for s in range(NT):
                        dve.tensor_scalar(diag[:, a, s, :], ident[:P, :P], elr[:, s, 2 * j + a:2 * j + a + 1], None,
                                          ALU.mult).then_inc(diag_ready, 1)

            take_z(0)
            dve.wait_ge(fs_ps, 1)
            dve.tensor_scalar(scales[:, 0:1], ps[:, 7, 0:1], 1.0 / (D * D), None, ALU.mult).then_inc(fscale, 1)
            diagonals(0)
            dve.wait_ge(fscale, 2)
            dve.tensor_scalar(scales[:, 1:2], scales[:, 0:1], 0.5, None, ALU.mult).then_inc(fscale, 1)
            dve.tensor_scalar(scales[:, 2:3], scales[:, 0:1], -0.5, None, ALU.mult).then_inc(fscale, 1)
            dve.wait_ge(fscale, 4)
            take_z(1)
            dve.wait_ge(z_used, (1 + Z_CH) * NT)
            diagonals(1)

            dve.sem_inc(k_ready, NT)
            dve.memset(v_sb[:, :, :, PAIR:PAIR + 1], 1.0).then_inc(ones_v, 1)
            dve.sem_inc(pr, 1)

            def phi(dst, round_, ci):
                def end(nt):
                    dve.wait_ge(k_exp, round_ * NT + (nt + 1))
                    dve.scalar_tensor_tensor(dst[:, nt, :], tmp[:, nt, :], 1.0, dst[:, nt, :],
                                             ALU.add, ALU.max).then_inc(k_ready, 1)

                for nt in range(NT):
                    dve.wait_ge(bank_free, (ci + NG) * NT + (nt + 1))
                    dve.tensor_scalar(dst[:, nt, :], tmp[:, nt, :], 0.0, None, ALU.min).then_inc(k_min, 1)
                    if nt >= 1:
                        end(nt - 1)
                end(NT - 1)

            def scores(u, j):
                a, dt = unit(u)
                un = j * UPS + u
                er = sm[:, u, 5:6]
                s0 = un * 6
                dve.tensor_scalar(er, elr[:, dt, ds(j * 2 + (HEADS + a), 1)], 0.0, None, ALU.add).then_inc(st, 1)
                dve.tensor_tensor_reduce(
                    out=score[:, u % 2, :], in0=no_edge[:, dt, :N],
                    in1=el_rows[:, a, :], scale=1.0, scalar=2 * NEG,
                    op0=ALU.add, op1=ALU.max, accum_out=sm[:, u, 0:1]).then_inc(st, 1)
                dve.wait_ge(st, s0 + 2)
                dve.tensor_scalar(sm[:, u, 1:2], sm[:, u, 0:1], er, NEG_FLOOR, ALU.add, ALU.max).then_inc(st, 1)
                dve.wait_ge(st, s0 + 3)
                dve.scalar_tensor_tensor(sm[:, u, 4:5], sm[:, u, 1:2], SLOPE, sm[:, u, 1:2],
                                         ALU.mult, ALU.max).then_inc(st, 1)
                dve.wait_ge(st, s0 + 4)
                dve.tensor_tensor(sm[:, u, 2:3], er, sm[:, u, 4:5], ALU.subtract).then_inc(st, 1)
                dve.scalar_tensor_tensor(sm[:, u, 3:4], er, SLOPE, sm[:, u, 4:5],
                                         ALU.mult, ALU.subtract).then_inc(st, 1)

            def probs(u, j):
                a, dt = unit(u)
                un = j * UPS + u
                dve.wait_ge(exps, un * 2 + 2)
                dve.tensor_tensor(exp_a[:], exp_a[:], exp_b[:], ALU.max).then_inc(pr, 1)
                dve.wait_ge(pr, un * 2 + 2)
                dve.tensor_tensor_reduce(out=prob[:, u % 2, :], in0=exp_a[:], in1=counts[:, dt, :N], scale=1.0,
                                         scalar=0.0, op0=ALU.mult, op1=ALU.add,
                                         accum_out=ssum[:, u:u + 1]).then_inc(pr, 1)

            def take(u, j):
                un = j * UPS + u
                dve.wait_ge(pt_hi_ready, un + 1)
                dve.tensor_tensor(pt_lo[:], pt_ps[:P, 0:NT, :P], pt_hi[:].bitcast(f32),
                                  ALU.subtract).then_inc(pt_ready, 1)

            def add_gat(u, j):
                a, dt = unit(u)
                un = j * UPS + u
                dve.tensor_scalar(rsum[:, u:u + 1], ssum[:, u:u + 1], 1e-30, None, ALU.max).then_inc(rs, 1)
                dve.wait_ge(rs, un * 2 + 1)
                dve.reciprocal(rsum[:, u:u + 1], rsum[:, u:u + 1]).then_inc(rs, 1)
                dve.wait_ge(rs, un * 2 + 2)
                dve.wait_ge(agg_done, un + 2)
                cols = ds(j * 2 * F + a * F, F)
                dve.scalar_tensor_tensor(x_sb[:, dt, cols], ps[:P, AGG, :F], rsum[:, u:u + 1],
                                         x_sb[:, dt, cols], ALU.mult, ALU.add).then_inc(agg_free, 1)

            with dve.Fori(0, 2) as j:
                dve.wait_ge(up, ups)
                dve.wait_ge(el_free, j * 2 + 2)
                scores(0, j)
                scores(1, j)
                probs(0, j)
                for u in range(UPS):
                    if UNIT_STEPS[u] == KT + 1:
                        phi(k_sb, j, j * 2 + Z_CH)
                    take(u, j)
                    if u + 2 < UPS:
                        scores(u + 2, j)
                    if u + 1 < UPS:
                        probs(u + 1, j)
                    add_gat(u, j)
                for b in range(2):
                    dve.wait_ge(kv_done, j * 2 + (b + 2))
                    dve.wait_ge(kv_zero, 1)
                    for h in range(2):
                        rws = slice(h * DK, (h + 1) * DK)
                        src = ps[rws, 5 + b, :2 * (PAIR + 1)].rearrange("p (r f) -> p r f", f=PAIR + 1)
                        dst = kv_blocks[rws, ds(j * HP + 2 * b, 2), :]
                        dve.tensor_copy(dst[:, :, h * DK:(h + 1) * DK], src[:, :, h * DK:(h + 1) * DK]).then_inc(kv_free, 1)
                        dve.tensor_copy(dst[:, :, PAIR + h:PAIR + h + 1], src[:, :, PAIR:PAIR + 1]).then_inc(kv_free, 1)

            def ternary(u):
                b, c, k = u % 2, u // KT, u % KT
                dve.wait_ge(f_in[b], 16 * ((NU + u) // 2 + 1))
                if u >= 2:
                    dve.wait_ge(f_tern, u - 1)
                dve.tensor_scalar(above[:, b, :], f_raw[:, b, :], scales[:, 1:2], None, ALU.is_gt,
                                  saturate=False).then_inc(f_above, 1)
                dve.wait_ge(f_above, u + 1)
                dve.scalar_tensor_tensor(tern[:, k, c * CH:(c + 1) * CH], f_raw[:, b, :], scales[:, 2:3],
                                         above[:, b, :], ALU.is_lt, ALU.subtract,
                                         saturate=False).then_inc(f_tern, 1)

            def q_ps(r, h):
                cols, kept = HALVES[h]
                return ps[:, 2 * (r % 2) + h, kept.start - cols.start:kept.stop - cols.start]

            for r in range(NPAIR):
                ternary(2 * r)
                ternary(2 * r + 1)
                for h, (_, kept) in enumerate(HALVES):
                    dve.wait_ge(q_done, 2 * r + h + 1)
                    dve.tensor_scalar(q_t[:, r, kept], q_ps(r, h), 0.0, None,
                                      ALU.min).then_inc(q_min, 1)
                for h, (_, kept) in enumerate(HALVES):
                    dve.wait_ge(q_exp, 2 * r + h + 1)
                    dve.scalar_tensor_tensor(q_t[:, r, kept], q_ps(r, h), 1.0,
                                             q_t[:, r, kept], ALU.add, ALU.max).then_inc(q_ready, 1)

            PB = [3, 3, 2]

            def attention(t):
                for b, n in enumerate(PB):
                    dve.wait_ge(num_done, 3 * t + b + 1)
                    src = ps[:P, 5 + b, :n * (PAIR + 2)].rearrange("p (r f) -> p r f", f=PAIR + 2)
                    dve.tensor_scalar(den[:, t % 2, 6 * b:6 * b + 2 * n].rearrange("p (r h) -> p r h", h=2),
                                      src[:, :, PAIR:PAIR + 2], DEN_EPS, None, ALU.add).then_inc(at_v, 1)
                dve.wait_ge(at_v, 4 * t + 3)
                dve.reciprocal(den[:, t % 2, :], den[:, t % 2, :]).then_inc(at_v, 1)
                dve.wait_ge(at_v, 4 * t + 4)
                if t >= 2:
                    dve.wait_ge(attn_t, 2 * (t - 1))
                for b, n in enumerate(PB):
                    for h in range(2):
                        src = ps[:P, 5 + b, :n * (PAIR + 2)].rearrange("p (r f) -> p r f", f=PAIR + 2)
                        dst = rows[:, t % 2, 3 * b * PAIR:(3 * b + n) * PAIR].rearrange("p (r f) -> p r f", f=PAIR)
                        dv = den[:, t % 2, 6 * b:6 * b + 2 * n].rearrange("p (r h) -> p r h", h=2)
                        dve.tensor_tensor(dst[:, :, h * DK:(h + 1) * DK], src[:, :, h * DK:(h + 1) * DK],
                                          dv[:, :, h:h + 1].broadcast_to([P, n, DK]), ALU.mult).then_inc(attn_ready, 1)

            def attn_split(t):
                for b in range(2):
                    dve.wait_ge(attn_hi, 2 * t + b + 1)
                    sl = (slice(None), slice(4 * b, 4 * b + 4), slice(t * P, (t + 1) * P))
                    dve.tensor_tensor(act_lo[sl], ps[:, 4 + b, :].rearrange("p (c q) -> p c q", q=128)[:, :, :P],
                                      act_hi[sl].bitcast(f32), ALU.subtract).then_inc(attn_lo, 1)

            def second_ln(t):
                n = X1S * t
                for c in range(2):
                    dve.wait_ge(wo_done, 2 * t + c + 1)
                    dve.tensor_tensor(x_sb[:, t, c * CH:(c + 1) * CH], ps[:P, 2 * (t % 2) + c, :],
                                      x_sb[:, t, c * CH:(c + 1) * CH], ALU.add).then_inc(x1, 1)
                dve.wait_ge(x1, n + 2)
                for h in range(2):
                    dve.bn_stats(bn[:, h, :], x_sb[:, t, h * CH:(h + 1) * CH]).then_inc(x1, 1)
                dve.wait_ge(x1, n + 4)
                dve.bn_aggr(mv[:], bn[:].rearrange("p a b -> p (a b)")).then_inc(x1, 1)
                dve.wait_ge(x1, n + 5)
                dve.tensor_scalar(ln[:, t, 0:1], mv[:, 1:2], LN_EPS, None, ALU.add).then_inc(x1, 1)
                dve.tensor_scalar(ln[:, t, 7:8], mv[:, 0:1], -1.0, None, ALU.mult).then_inc(x1, 1)
                dve.wait_ge(centred_in, t + 1)
                dve.tensor_reduce(ln[:, t, 8:9], centred[:, t, :], axis=AX.X, op=ALU.max,
                                  apply_absolute_value=True).then_inc(x1, 1)
                dve.wait_ge(ln_std, NT + t + 1)
                for i in range(5):
                    rstd_step(i, ln[:, t, :], x1, n + 8)
                dve.wait_ge(x1, n + 13)
                dve.tensor_tensor(amax[:, t:t + 1], ln[:, t, 8:9], ln[:, t, 6:7], ALU.mult).then_inc(x1, 1)

            attention(0)
            attn_split(0)
            for t in range(NT):
                if t + 1 < NT:
                    attention(t + 1)
                    attn_split(t + 1)
                second_ln(t)

            dve.wait_ge(x1, X1S * NT)
            dve.reduce_max(amax[:, NT:NT + 1], amax[:, :NT], axis=AX.X).then_inc(gm, 1)
            dve.wait_ge(gm_ps, 1)
            dve.reduce_max(gmax[:], ps[0:1, 4, :P], axis=AX.X).then_inc(gm, 1)
            dve.wait_ge(gm_ps, 2)
            dve.tensor_scalar(scales[:P, 3:4], ps[:P, 5, 0:1], 1.0 / 127.0, None, ALU.mult).then_inc(gm, 1)
            dve.wait_ge(gm, 3)
            dve.reciprocal(scales[:P, 4:5], scales[:P, 3:4]).then_inc(quant, 1)
            dve.scalar_tensor_tensor(scales[:P, 5:6], scales[:P, 3:4], -1.0, scales[:P, 0:1],
                                     ALU.mult, ALU.mult).then_inc(quant, 1)
            dve.wait_ge(quant, 2)
            dve.tensor_scalar(ln[:, :, 5], ln[:, :, 6], scales[:P, 4:5], None, ALU.mult).then_inc(quant, 1)
            dve.wait_ge(quant, 3)

            def quantise(t):
                dve.tensor_scalar(rows[:, t % 2, :], centred[:, t, :], ln[:, t, 5:6], 127.0,
                                  ALU.mult, ALU.min).then_inc(quant, 1)
                dve.wait_ge(quant, 3 + 2 * t + 1)
                dve.tensor_scalar(rows[:, t % 2, :], rows[:, t % 2, :], -128.0, MAGIC, ALU.max, ALU.add).then_inc(quant, 1)

            def finish(t):
                dve.wait_ge(biased, t + 1)
                for c in range(2):
                    dve.wait_ge(ffn_done, 2 * t + c + 1)
                    dve.scalar_tensor_tensor(x_sb[:, t, c * CH:(c + 1) * CH], ps[:P, 2 * (t % 2) + c, :],
                                             scales[:P, 5:6], x_sb[:, t, c * CH:(c + 1) * CH],
                                             ALU.mult, ALU.add).then_inc(y_ready, 1)

            quantise(0)
            quantise(1)
            for t in range(NT):
                if t + 2 < NT:
                    dve.wait_ge(quant_ps, 2 * (t + 1))
                    quantise(t + 2)
                finish(t)

        @block.tensor
        def _(pe):
            def three_pass(dst, a, b, first, last):
                pe.matmul(dst, a[0], b[0], start=first, stop=False)
                pe.matmul(dst, a[0], b[1], start=False, stop=False)
                return pe.matmul(dst, a[1], b[0], start=False, stop=last)

            def row_transposes(n):
                pe.wait_ge(row_ready, n + 1)
                for b in range(2):
                    if n > 0:
                        pe.wait_ge(row_t_in, 2 * (n - 1) + b + 1)
                    for c in range(4):
                        last = pe.transpose(pt_ps[:, 4 * b + c, :P],
                                            rows[:, n % 2, (4 * b + c) * 128:(4 * b + c + 1) * 128], ident[:P, :P])
                    last.then_inc(row_t, 1)

            def count(half, end):
                with pe.Fori(half, end) as q:
                    for s in range(RING):
                        pe.wait_ge(oh_ready, q * (2 * RING) + (2 * s + 2))
                        for nt in range(NT):
                            last = pe.matmul(ps[:P, nt, :HALF], onehot_dst[:, s, nt * P:(nt + 1) * P],
                                             onehot_src[:, s, :], start=False, stop=False)
                        last.then_inc(oh_used, 1)

            pe.sem_inc(oh_used, RING)
            pe.wait_ge(consts, 5)
            for g, segs in enumerate(GROUP_SEGS):
                for nt in range(NT):
                    if g > 0:
                        pe.wait_ge(bank_free, (g - 1) * NT + nt + 1)
                    pe.matmul(ps[:P, nt, :HALF], zeros[:], iota[:, :HALF], start=True, stop=False)
                for n in segs:
                    if n >= 1:
                        row_transposes(n - 1)
                    if n < NT - 1:
                        count(2 * n, 2 * n + 2)
                    else:
                        count(2 * n, 2 * n + 1)
                        row_transposes(n)
                        count(2 * n + 1, 2 * n + 2)
                    if n == segs[-1]:
                        for nt in range(NT):
                            pe.matmul(ps[:P, nt, :HALF], zeros[:], iota[:, :HALF], start=False,
                                      stop=True).then_inc(count_done, 1)
            pe.wait_ge(act_ready, 2 * NT)

            def step(ci, k, unit_no, slot):
                pe.wait_ge(w_ready, unit_no)
                for nt in range(NT):
                    if k == 0:
                        pe.wait_ge(bank_free, (ci + NG - 1) * NT + (nt + 1))
                    rws = slice(nt * P, (nt + 1) * P)
                    last = three_pass(ps[:P, nt, :], (act_hi[:, k, rws], act_lo[:, k, rws]),
                                      (w_hi[:, slot, :], w_lo[:, slot, :]), k == 0, k == KT - 1)
                    if k == KT - 1:
                        last.then_inc(proj_done, 1)
                if k < KT - 1:
                    last.then_inc(w_used, 1)

            pe.wait_ge(fscale, 1)
            pe.matmul(ps[:, 7, 0:1], ones[:], abs_sum[:, NU:NU + 1], start=True, stop=True).then_inc(fs_ps, 1)

            with pe.Fori(0, Z_CH) as c:
                for k in range(KT):
                    step(c, k, c * KT + (k + 1), k % QUAD)

            pe.sem_inc(kv_done, 1)
            pe.sem_inc(agg_done, 1)
            pe.sem_inc(agg_free, 1)
            pe.sem_inc(kv_free, 1)
            with pe.Fori(0, 2) as j:
                for g in range(2 * KT):
                    u = UNIT_STEPS.index(g) if g in UNIT_STEPS else None
                    if u is not None:
                        a, dt = unit(u)
                        un = j * UPS + u
                        pe.wait_ge(pr, un * 2 + 3)
                        for s in range(NT):
                            last = pe.transpose(pt_ps[:P, s, :P], prob[:, u % 2, s * P:(s + 1) * P], ident[:P, :P])
                        last.then_inc(pt_done, 1)
                    ci = j * 2 + (Z_CH + g // KT)
                    step(ci, g % KT, ci * KT + (g % KT + 1), g % QUAD)
                    if g == EL_STEP:
                        for a in range(2):
                            pe.wait_ge(diag_ready, j * (2 * NT) + (a * NT + NT))
                            if a == 0:
                                pe.wait_ge(kv_free, j * 8 + 1)
                            else:
                                pe.wait_ge(agg_free, j * UPS + 1)
                                pe.wait_ge(fscale, 2)
                            for s in range(NT):
                                last = pe.matmul(pt_ps[:P, a * NT + s, :P], ones[:P, :P], diag[:, a, s, :],
                                                 start=True, stop=True)
                            last.then_inc(el_ps, 1)
                    if u is not None:
                        pe.wait_ge(pt_ready, un + 1)
                        pe.wait_ge(agg_free, un + 1)
                        cols = ds(j * 2 * F + a * F, F)
                        for s in range(NT):
                            last = three_pass(ps[:P, AGG, :F], (pt_hi[:, s, :], pt_lo[:, s, :]),
                                              (z_hi[:, s, cols], z_lo[:, s, cols]), s == 0, s == NT - 1)
                        last.then_inc(agg_done, 1)
                pe.wait_ge(bank_free, (j * 2 + (Z_CH + 1 + NG)) * NT + NT)
                pe.wait_ge(k_ready, j * NT + 2 * NT)
                for b in range(2):
                    for r in range(2):
                        pr_ = 2 * b + r
                        for nt in range(NT):
                            last = pe.matmul(ps[:, 5 + b, r * (PAIR + 1):(r + 1) * (PAIR + 1)],
                                             k_sb[:, nt, pr_ * PAIR:(pr_ + 1) * PAIR], v_sb[:, nt, pr_, :],
                                             start=nt == 0, stop=nt == NT - 1)
                    last.then_inc(kv_done, 1)

            for i in range(NU):
                r, slot = i // 2, i % QUAD
                pe.wait_ge(w_ready, stream_q(i) + 1)
                for c in range(4):
                    k = 4 * (i % 2) + c
                    blk = slice(c * 128, (c + 1) * 128)
                    for h, (cols, _) in enumerate(HALVES):
                        if k == 0 and r >= 2:
                            pe.wait_ge(q_ready, 2 * (r - 2) + h + 1)
                        last = three_pass(ps[:, 2 * (r % 2) + h, :cols.stop - cols.start], (w_hi[:, slot, blk], w_lo[:, slot, blk]),
                                          (act_hi[:, k, cols], act_lo[:, k, cols]), k == 0, k == KT - 1)
                        if k == KT - 1:
                            last.then_inc(q_done, 1)
                if i % 2 == 0:
                    last.then_inc(w_used, 1)

            def numerator(t):
                for r in range(NPAIR):
                    b, i = r // 3, r % 3
                    if t == 0:
                        pe.wait_ge(q_ready, 2 * r + 1)
                    elif r == 0 and t == 1:
                        pe.wait_ge(q_ready, 2 * NPAIR)
                    last = pe.matmul(ps[:P, 5 + b, i * (PAIR + 2):(i + 1) * (PAIR + 2)],
                                     q_t[:, r, t * P:(t + 1) * P], kv_blocks[:, r, :], start=True, stop=True)
                    if i == 2 or r == NPAIR - 1:
                        last.then_inc(num_done, 1)

            def attn_transposes(t):
                for b in range(2):
                    pe.wait_ge(attn_ready, 6 * (t + 1))
                    for c in range(4):
                        last = pe.transpose(ps[:, 4 + b, c * 128:c * 128 + P],
                                            rows[:, t % 2, (4 * b + c) * 128:(4 * b + c + 1) * 128], ident[:P, :P])
                    last.then_inc(attn_t, 1)

            pe.wait_ge(kv_free, 2 * 8 + 1)
            numerator(0)
            attn_transposes(0)
            for t in range(NT):
                if t + 1 < NT:
                    pe.wait_ge(attn_lo, 2 * (t + 1))
                    numerator(t + 1)
                for c in range(2):
                    for k in range(KT):
                        if t == 0:
                            pe.wait_ge(w_ready, stream_o(c * KT + k) + 1)
                        if k == 0:
                            pe.wait_ge(attn_lo, 2 * (t + 1))
                            if t >= 2:
                                pe.wait_ge(x1, X1S * (t - 2) + c + 1)
                        rws, cols = slice(t * P, (t + 1) * P), slice(c * CH, (c + 1) * CH)
                        last = three_pass(ps[:P, 2 * (t % 2) + c, :], (act_hi[:, k, rws], act_lo[:, k, rws]),
                                          (wo_hi[:, k, cols], wo_lo[:, k, cols]), k == 0, k == KT - 1)
                    last.then_inc(wo_done, 1)
                    if c == 0 and t + 1 < NT:
                        attn_transposes(t + 1)

            pe.wait_ge(gm, 1)
            pe.transpose(ps[0:1, 4, :P], amax[:, NT:NT + 1], ident[:P, :P]).then_inc(gm_ps, 1)
            pe.wait_ge(gm, 2)
            pe.matmul(ps[:P, 5, 0:1], ones[0:1, :P], gmax[:], start=True, stop=True).then_inc(gm_ps, 1)

            def quant_transposes(t):
                pe.wait_ge(quant, 3 + 2 * (t + 1))
                for b in range(2):
                    if t > 0:
                        pe.wait_ge(quant_ready, 2 * (t - 1) + b + 1)
                    for c in range(4):
                        last = pe.transpose(ps[:, 6 + b, c * 128:c * 128 + P],
                                            rows[:, t % 2, (4 * b + c) * 128:(4 * b + c + 1) * 128], ident[:P, :P])
                    last.then_inc(quant_ps, 1)

            quant_transposes(0)
            pe.wait_ge(f_tern, NU)
            for t in range(NT):
                if t + 1 < NT:
                    quant_transposes(t + 1)
                pe.wait_ge(quant_ready, 2 * (t + 1))
                for c in range(2):
                    if t >= 2:
                        pe.wait_ge(y_ready, 2 * (t - 2) + c + 1)
                    for k in range(KT):
                        last = pe.matmul(ps[:P, 2 * (t % 2) + c, :], quant_t[:, t % 2, k, :P],
                                         tern[:, k, c * CH:(c + 1) * CH], start=k == 0, stop=k == KT - 1)
                    last.then_inc(ffn_done, 1)


def _units(w):
    rows, cols = w.shape
    return w.reshape(rows // 128, 128, cols // 512, 512).transpose(2, 0, 1, 3).reshape(-1, 128, 512)


def _lay_out(src, dst, W, a_l, a_r, w_qkv, w_o, weight):
    import numpy as np

    heads, d, f = W.shape
    z = _units(W.transpose(1, 0, 2).reshape(d, heads * f))
    k, v = (_units(w_qkv[:, i * d:(i + 1) * d]) for i in (1, 2))
    q = w_qkv[:, :d].reshape(2, 4, 128, d // 128, 128).transpose(3, 0, 2, 1, 4).reshape(-1, 128, 512)
    o = _units(w_o)
    h = len(k) // 2
    first = 4
    mixed = [q[:first]]
    for i in range(len(o)):
        mixed.append(o[i:i + 1])
        if i + first < len(q):
            mixed.append(q[i + first:i + first + 1])
    weights = np.concatenate([z, k[:h], v[:h], k[h:], v[h:], *mixed])
    return {
        "edges": np.stack([src, dst]),
        "a_lr": np.stack([a_l.reshape(-1), a_r.reshape(-1)]),
        "weights": weights,
        "ffn_weights": _units(weight.T),
    }


def kernel(x, src, dst, L0_gnn_W, L0_gnn_a_l, L0_gnn_a_r, L0_mix_w_qkv, L0_mix_w_o, L0_ffn_weight, L0_ffn_bias):
    import numpy as np
    import concourse.bacc as bacc
    from concourse.bass_utils import run_bass_kernel_spmd

    arrays = {"x": np.asarray(x)}
    arrays.update(_lay_out(*(np.asarray(a) for a in (src, dst, L0_gnn_W, L0_gnn_a_l, L0_gnn_a_r,
                                                     L0_mix_w_qkv, L0_mix_w_o, L0_ffn_weight))))
    arrays["bias"] = np.asarray(L0_ffn_bias)
    nc = bacc.Bacc("TRN2", target_bir_lowering=False, num_devices=1)
    arrays = {f"in_{k}": np.ascontiguousarray(v) for k, v in arrays.items()}
    args = [nc.dram_tensor(k, v.shape, mybir.dt.from_np(v.dtype), kind="ExternalInput").ap()
            for k, v in arrays.items()]
    out = nc.dram_tensor("out_0", x.shape, mybir.dt.float32, kind="ExternalOutput").ap()
    gps_layer(nc, *args, out)
    result = run_bass_kernel_spmd(nc, [arrays], core_ids=[0])
    return result.results[0]["out_0"]
```

```python
import concourse.bass as bass
from concourse import mybir
from contextlib import ExitStack


def gps_layer(nc, x, edges, a_lr, weights, ffn_weights, bias, out):
    f32, f32r, bf16 = mybir.dt.float32, mybir.dt.float32r, mybir.dt.bfloat16
    f16, i16, i32, fp8 = mybir.dt.float16, mybir.dt.int16, mybir.dt.int32, mybir.dt.float8e4
    ALU, ACT = mybir.AluOpType, mybir.ActivationFunctionType
    AX = mybir.AxisListType
    ds = bass.ds

    N, D = x.shape
    P = 125
    NT = N // P
    KT = D // 128
    HEADS, F = 4, 256
    CH = 512
    DK, PAIR = 64, 128
    NPAIR = D // PAIR
    HP = NPAIR // 2
    E = edges.shape[1]
    ET = E // P
    SEG = ET // NT
    RING = SEG // 2
    STATS = 8
    QUAD = 4
    HALF = (N + 1) // 2 + 1
    NPAD = 2 * ((N + 1) // 2)
    BASE = 4096
    GROUP_SEGS = [(0, 1), (2, 3), (4,)]
    NG = len(GROUP_SEGS)
    assert max(len(g) for g in GROUP_SEGS) * SEG * P < BASE and NT * P == N and ET * P == E
    MAGIC = 12582912.0
    NEG = -1.0e38
    NEG_FLOOR = -4.0e37
    SLOPE, LN_EPS, DEN_EPS = 0.2, 1e-5, 1e-6
    Z_CH, KV_CH = 2, 4
    N1 = N // 2 // 2 * 2
    HALVES = [(slice(0, N1), slice(0, N1)), (slice(N1 - N % 2, N), slice(N1, N))]
    ELS = 4
    RQ = (Z_CH + KV_CH) * KT
    UPS = 2 * NT
    NU = D // CH * KT

    ctx = ExitStack()
    with ctx:
        base = (nc.sbuf_base + 31) // 32 * 32
        AREA = 60480
        RAW, WHI, WLO = 126016, 134208, 142400
        KVO, CNT, MSK, ELB, GAT = 150592, 154752, 161024, 167296, 172320
        PHI, TERN, TMP, FRAW, IOTA, END = 174752, 184992, 193184, 203424, 207520, 208800
        ctx.enter_context(nc.sbuf_tensor("arena", [128, END], mybir.dt.uint8))

        def at(name, shape, dtype, offset):
            return nc.alloc_sbuf_tensor_at(name, shape, dtype, offset=base + offset)

        def sb(name, shape, dtype=f32):
            return ctx.enter_context(nc.sbuf_tensor(name, shape, dtype))

        x_sb = at("x_sb", [P, NT, D], f32, 0)
        act_hi = at("act_hi", [128, KT, N], f32r, 20480)
        act_lo = at("act_lo", [128, KT, N], f32r, 40480)
        z_hi = at("z_hi", [P, NT, D], f32r, AREA)
        z_lo = at("z_lo", [P, NT, D], f32r, AREA + 20480)
        k_sb = at("k_sb", [P, NT, CH], f32, AREA + 40960)
        v_sb = at("v_sb", [P, NT, HP, PAIR + 1], f32, AREA + 51200)
        onehot_dst = at("onehot_dst", [P, RING, NPAD], bf16, AREA)
        onehot_src = at("onehot_src", [P, RING, HALF], bf16, AREA + 20032)
        csum = at("csum", [P, NT, HALF], f32, AREA + 32768)
        row_t_sb = at("row_t_sb", [128, 2, 4, P], f32, AREA + 40960)
        alr = at("alr", [P, 2, D], f32, AREA + 48512)
        edge_i = at("edge_i", [P, 2, ET], i32, AREA + 56704)
        half_i = at("half_i", [P, 2, ET], i32, AREA + 57344)
        dst_f = at("dst_f", [P, ET], f32, AREA + 57984)
        src_half = at("src_half", [P, ET], f32, AREA + 58304)
        src_worth = at("src_worth", [P, ET], f32, AREA + 58624)
        wo_hi = at("wo_hi", [128, KT, D], f32r, AREA)
        wo_lo = at("wo_lo", [128, KT, D], f32r, AREA + 32768)
        w_raw = at("w_raw", [128, QUAD, CH], f32, RAW)
        w_hi = at("w_hi", [128, QUAD, CH], f32r, WHI)
        w_lo = at("w_lo", [128, QUAD, CH], f32r, WLO)
        tern = at("tern", [128, KT, D], fp8, TERN)
        kv_blocks = at("kv_blocks", [128, NPAIR, PAIR + 2], f32, KVO)
        counts = at("counts", [P, NT, NPAD], i16, CNT)
        no_edge = at("no_edge", [P, NT, NPAD], bf16, MSK)
        el_rows = at("el_rows", [P, 2, N], f32, ELB)
        q_t = at("q_t", [128, NPAIR, N], f32, CNT)
        packed = at("packed", [P, NG, NT, HALF], f32, GAT)
        score = at("score", [P, 2, N], f32, GAT)
        exp_a = at("exp_a", [P, N], f32, GAT + 5024)
        exp_b = at("exp_b", [P, N], f32, GAT + 7552)
        prob = at("prob", [P, 2, N], f32, GAT + 10080)
        pt_hi = at("pt_hi", [P, NT, P], f32r, GAT + 15104)
        pt_lo = at("pt_lo", [P, NT, P], f32r, GAT + 17632)
        diag = at("diag", [P, 2, NT, P], f32, FRAW)
        quant_rows = at("quant_rows", [P, 2, D], bf16, AREA)
        junk = at("junk", [P, ELS, F], f32, GAT)
        centred = at("centred", [P, NT, D], f32, RAW)
        f_raw = at("f_raw", [128, 2, CH], f32, FRAW)
        above = at("above", [128, 2, CH], fp8, IOTA)
        bias_sb = at("bias_sb", [P, D], f32, PHI)
        quant_t = at("quant_t", [128, 2, KT, 128], bf16, PHI + 4096)
        tmp = at("tmp", [P, NT, CH], f32, TMP)
        unpack = at("unpack", [P, NT, HALF], f32, TMP)
        rows = at("rows", [P, 2, D], f32, TMP)

        iota = at("iota", [P, NPAD], f16, IOTA)
        ident = sb("ident", [128, 128])
        ident_bf = sb("ident_bf", [128, 128], bf16)
        ones = sb("ones", [128, 128])
        zeros = sb("zeros", [P, CH], f16)
        bn = sb("bn", [P, 4, 6])
        mv = sb("mv", [P, 2])
        ln = sb("ln", [P, NT, 9])
        elr = sb("elr", [P, NT, 2 * HEADS])
        sm = sb("sm", [P, UPS, 6])
        ssum = sb("ssum", [P, UPS])
        rsum = sb("rsum", [P, UPS])
        den = sb("den", [P, 2, 2 * NPAIR])
        amax = sb("amax", [P, NT])
        extremes = sb("extremes", [P, NT, 6])
        abs_sum = sb("abs_sum", [128, NU + 1])
        scales = sb("scales", [128, 8])

        ps = ctx.enter_context(nc.psum_tensor("ps", [128, 8, 512], f32))
        pt_ps = ps[:, 5:8, :].rearrange("p b (c q) -> p (b c) q", q=128)
        AGG = 7

        def sem(name):
            return ctx.enter_context(nc.semaphore(name))

        edges_in, alr_in, bias_in = sem("edges_in"), sem("alr_in"), sem("bias_in")
        row_t_in = sem("row_t_in")
        x_in = [sem(f"x_in{t}") for t in range(NT)]
        raw_in = [sem(f"raw_in{s}") for s in range(QUAD)]
        f_in = [sem(f"f_in{s}") for s in range(2)]
        consts = sem("consts")
        zeros_in = sem("zeros_in")
        kv_zero = sem("kv_zero")
        idx = sem("idx")
        oh_ready, oh_used = sem("oh_ready"), sem("oh_used")
        count_done = sem("count_done")
        bank_free = sem("bank_free")
        ln_a, ln_std = sem("ln_a"), sem("ln_std")
        row_mid, row_ready, row_t = sem("row_mid"), sem("row_ready"), sem("row_t")
        act_ready = sem("act_ready")
        up = sem("up")
        w_hi_ready, w_ready = sem("w_hi_ready"), sem("w_ready")
        w_used = sem("w_used")
        proj_done = sem("proj_done")
        z_hi_ready, z_used = sem("z_hi_ready"), sem("z_used")
        el = sem("el")
        diag_ready = sem("diag_ready")
        el_ps, el_free = sem("el_ps"), sem("el_free")
        st = sem("st")
        exps = sem("exps")
        pr = sem("pr")
        pt_done, pt_hi_ready, pt_ready = sem("pt_done"), sem("pt_hi_ready"), sem("pt_ready")
        agg_done, agg_free = sem("agg_done"), sem("agg_free")
        rs = sem("rs")
        k_min, k_exp, k_ready = sem("k_min"), sem("k_exp"), sem("k_ready")
        q_done, q_min, q_exp, q_ready = sem("q_done"), sem("q_min"), sem("q_exp"), sem("q_ready")
        ones_v, kv_done, kv_free = sem("ones_v"), sem("kv_done"), sem("kv_free")
        f_abs, fscale, fs_ps = sem("f_abs"), sem("fscale"), sem("fs_ps")
        f_above, f_tern = sem("f_above"), sem("f_tern")
        num_done, at_den, at_rec, attn_ready = sem("num_done"), sem("at_den"), sem("at_rec"), sem("attn_ready")
        attn_t, attn_hi, attn_lo = sem("attn_t"), sem("attn_hi"), sem("attn_lo")
        wo_done, x1, centred_in = sem("wo_done"), sem("x1"), sem("centred_in")
        ln_b, ln_p = sem("ln_b"), sem("ln_p")
        gm, gm_ps = sem("gm"), sem("gm_ps")
        held, quant, rounded = sem("held"), sem("quant"), sem("rounded")
        quant_ps, quant_ready = sem("quant_ps"), sem("quant_ready")
        biased, ffn_done, y_ready, stored = sem("biased"), sem("ffn_done"), sem("y_ready"), sem("stored")

        LNS, LNB = 9, 10
        PARTS = [(0, CH), (CH, D)]
        LAST_PARTS = [(0, CH), (CH, CH + CH // 2), (CH + CH // 2, D)]
        NUNIT = HEADS * NT
        UNIT_STEPS = [5, 6, 7, 9, 10, 11, 12, 13, 14, 15]
        PHI_UNIT = UNIT_STEPS.index(KT + 1)
        EL_STEP = 1

        def unit(u):
            return u // NT, u % NT

        def stream_q(i):
            return RQ + i if i < QUAD else RQ + QUAD + 2 * (i - QUAD) + 1

        def stream_o(i):
            return RQ + QUAD + 2 * i if i < NU - QUAD else RQ + NU + i

        NSTREAM = RQ + 2 * NU
        EARLY = RQ + QUAD

        PB = [3, 3, 2]

        def parts_of(t):
            return LAST_PARTS if t == NT - 1 else PARTS

        def part_bank(t, i):
            return 2 * (t % 2) + i

        def quant_bank(b):
            return ps[:, 6 + b, :256].bitcast(bf16)

        block = ctx.enter_context(nc.Block())

        @block.sync
        def _(sp):
            sp.dma_start(edge_i[:], edges.rearrange("a (p t) -> p a t", p=P)).then_inc(edges_in, 16)
            for t in range(NT):
                sp.dma_start(x_sb[:, t, :], x[t * P:(t + 1) * P, :]).then_inc(x_in[t], 16)
            for s in range(QUAD):
                sp.dma_start(w_raw[:, s, :], weights[s]).then_inc(raw_in[s], 16)
            sp.dma_start(alr[:], bass.AP(a_lr.tensor, 0, [[0, P], [1, 2 * D]])).then_inc(alr_in, 16)

            def load_quad(q):
                for s in range(QUAD):
                    sp.wait_ge(w_ready, q * QUAD + (s + 1 - QUAD))
                    sp.dma_start(w_raw[:, s, :], weights[ds(q * QUAD + s, 1)].rearrange("a p n -> p (a n)"))\
                      .then_inc(raw_in[s], 16)

            for s in range(2):
                sp.dma_start(f_raw[:, s, :], ffn_weights[s]).then_inc(f_in[s], 16)
            with sp.Fori(1, NU // 2) as h:
                for s in range(2):
                    sp.wait_ge(f_abs, h * 2 + (s - 1))
                    sp.dma_start(f_raw[:, s, :], ffn_weights[ds(h * 2 + s, 1)].rearrange("a p n -> p (a n)"))\
                      .then_inc(f_in[s], 16)
            QA = EARLY // QUAD + 1
            assert QA % 2 == 0 and NSTREAM % (2 * QUAD) == 0
            with sp.Fori(1, QA) as q:
                load_quad(q)
            for s in range(2):
                sp.wait_ge(el_ps, 2 * 2)
                sp.dma_start(f_raw[:, s, :], ffn_weights[s]).then_inc(f_in[s], 16)
            with sp.Fori(QA // 2, NSTREAM // QUAD // 2) as h:
                for s in range(2):
                    load_quad(h * 2 + s)
                    u = h * 2 + (s + 2 - QA)
                    sp.wait_ge(f_tern, u - 1)
                    sp.dma_start(f_raw[:, s, :], ffn_weights[ds(u, 1)].rearrange("a p n -> p (a n)"))\
                      .then_inc(f_in[s], 16)
            for u in range(2 + NSTREAM // QUAD - QA, NU):
                sp.wait_ge(f_tern, u - 1)
                sp.dma_start(f_raw[:, u % 2, :], ffn_weights[u]).then_inc(f_in[u % 2], 16)
            sp.wait_ge(q_done, 1)
            sp.dma_start(bias_sb[:], bass.AP(bias.tensor, 0, [[0, P], [1, D]])).then_inc(bias_in, 16)
            for t in range(NT):
                for i, (lo, hi) in enumerate(parts_of(t)):
                    sp.wait_ge(y_ready, 2 * t + i + 1)
                    sp.dma_start(out[t * P:(t + 1) * P, lo:hi], x_sb[:, t, lo:hi]).then_inc(stored, 16)
            sp.wait_ge(stored, 16 * (2 * NT + 1))

        @block.gpsimd
        def _(pool):
            pool.memset(zeros[:], 0.0).then_inc(zeros_in, 1)
            pool.iota(iota[:], [[1, NPAD]], base=0, channel_multiplier=0,
                      allow_small_or_imprecise_dtypes=True).then_inc(consts, 1)
            pool.memset(ones[:], 1.0).then_inc(consts, 1)
            pool.memset(ident[:], 0.0).then_inc(consts, 1)
            pool.wait_ge(consts, 3)
            pool.affine_select(out=ident[:], in_=ident[:], compare_op=ALU.not_equal, fill=1.0, base=0,
                               pattern=[[-1, 128]], channel_multiplier=1).then_inc(consts, 1)
            pool.memset(kv_blocks[:], 0.0).then_inc(kv_zero, 1)

            def lo_quad(q):
                for s in range(QUAD):
                    pool.wait_ge(w_hi_ready, q * QUAD + (s + 1))
                    pool.tensor_tensor(w_lo[:, s, :], w_raw[:, s, :], w_hi[:, s, :].bitcast(f32),
                                       ALU.subtract).then_inc(w_ready, 1)

            lo_quad(0)
            for t in range(NT):
                for b in range(2):
                    pool.wait_ge(row_t_in, 2 * t + b + 1)
                    sl = (slice(None), slice(4 * b, 4 * b + 4), slice(t * P, (t + 1) * P))
                    pool.tensor_tensor(act_lo[sl], row_t_sb[:, b, :, :], act_hi[sl].bitcast(f32),
                                       ALU.subtract).then_inc(act_ready, 1)
            with pool.Fori(1, EARLY // QUAD) as q:
                lo_quad(q)

            def lo_q(i):
                pool.wait_ge(w_hi_ready, stream_q(i) + 1)
                pool.tensor_tensor(w_lo[:, i % QUAD, :], w_raw[:, stream_q(i) % QUAD, :],
                                   w_hi[:, i % QUAD, :].bitcast(f32), ALU.subtract).then_inc(w_ready, 1)

            def lo_o(i):
                c, k = i // KT, i % KT
                pool.wait_ge(w_hi_ready, stream_o(i) + 1)
                pool.tensor_tensor(wo_lo[:, k, c * CH:(c + 1) * CH], w_raw[:, stream_o(i) % QUAD, :],
                                   wo_hi[:, k, c * CH:(c + 1) * CH].bitcast(f32),
                                   ALU.subtract).then_inc(w_ready, 1)

            for i in range(NU):
                lo_o(i)
                if i + QUAD < NU:
                    lo_q(i + QUAD)
            pool.wait_ge(bias_in, 16)
            for t in range(NT):
                pool.wait_ge(centred_in, t + 1)
                pool.tensor_tensor(x_sb[:, t, :], x_sb[:, t, :], bias_sb[:], ALU.add).then_inc(biased, 1)

        @block.scalar
        def _(act):
            def hi_unit(slot):
                act.activation(w_hi[:, slot, :], w_raw[:, slot, :], ACT.Copy).then_inc(w_hi_ready, 1)

            def row(t):
                act.wait_ge(ln_a, LNS * t + 5)
                act.activation(ln[:, t, 1:2], ln[:, t, 0:1], ACT.Sqrt).then_inc(ln_std, 1)
                if t >= 2:
                    act.wait_ge(row_t, 2 * (t - 1))
                act.activation(rows[:, t % 2, :], x_sb[:, t, :], ACT.Identity, bias=ln[:, t, 7:8]).then_inc(row_mid, 1)
                act.wait_ge(row_mid, t + 1)
                act.wait_ge(ln_a, LNS * (t + 1))
                act.activation(rows[:, t % 2, :], rows[:, t % 2, :], ACT.Identity, scale=ln[:, t, 6:7])\
                   .then_inc(row_ready, 1)

            def split_rows(t):
                for b in range(2):
                    src = pt_ps[:, 4 * b:4 * b + 4, :P]
                    act.wait_ge(row_t, 2 * t + b + 1)
                    act.activation(act_hi[:, 4 * b:4 * b + 4, t * P:(t + 1) * P], src, ACT.Copy)
                    if t >= 1:
                        act.wait_ge(act_ready, 2 * (t - 1) + b + 1)
                    act.activation(row_t_sb[:, b, :, :], src, ACT.Copy).then_inc(row_t_in, 1)

            def copy_counts(g):
                for nt in range(NT):
                    act.wait_ge(count_done, g * NT + nt + 1)
                    act.activation(packed[:, g, nt, :], ps[:P, nt, :HALF], ACT.Copy).then_inc(bank_free, 1)

            def abs_of(pair):
                for u in (2 * pair, 2 * pair + 1):
                    act.wait_ge(f_in[u % 2], 16 * (u // 2 + 1))
                    act.activation(f_raw[:, u % 2, :], f_raw[:, u % 2, :], ACT.Abs,
                                   accum_out=abs_sum[:, u:u + 1]).then_inc(f_abs, 1)

            row(0)
            for s in range(QUAD):
                act.wait_ge(raw_in[s], 16)
                hi_unit(s)
            row(1)
            abs_of(0)
            for t in range(NT):
                split_rows(t)
                if t + 2 < NT:
                    abs_of(t * 2 + 1)
                    row(t + 2)
                    abs_of(t * 2 + 2)
                elif t + 2 == NT:
                    abs_of(NU // 2 - 1)
                if t in (0, 2):
                    copy_counts(t // 2)
            copy_counts(2)

            def step_split(ci, k, q):
                s = k % QUAD
                act.wait_ge(raw_in[s], q * 16 + 16)
                if k < KT - 1:
                    act.wait_ge(w_used, ci * (KT - 1) + (k + 1))
                else:
                    act.wait_ge(proj_done, ci * NT + NT)
                hi_unit(s)

            with act.Fori(0, Z_CH) as c:
                for k in range(KT - 1):
                    step_split(c, k, c * 2 + (k // QUAD + 1))
                for nt in range(NT):
                    act.wait_ge(proj_done, c * NT + (nt + 1))
                    act.wait_ge(z_used, c * NT + (nt + 1))
                    act.activation(tmp[:, nt, :], ps[:P, nt, :], ACT.Copy).then_inc(bank_free, 1)
                step_split(c, KT - 1, c * 2 + 2)
                for nt in range(NT):
                    act.wait_ge(bank_free, (c + NG) * NT + (nt + 1))
                    act.activation(z_hi[:, nt, ds(c * CH, CH)], tmp[:, nt, :], ACT.Copy).then_inc(z_hi_ready, 1)

            def copy_k(j):
                for nt in range(NT):
                    act.wait_ge(proj_done, (j * 2 + Z_CH) * NT + (nt + 1))
                    act.wait_ge(k_ready, j * NT + (nt + 1))
                    act.activation(tmp[:, nt, :], ps[:P, nt, :], ACT.Copy).then_inc(bank_free, 1)

            def exp_k(j):
                for nt in range(NT):
                    act.wait_ge(k_min, j * NT + (nt + 1))
                    act.activation(k_sb[:, nt, :], k_sb[:, nt, :], ACT.Exp).then_inc(k_exp, 1)

            def exps_of(u, un):
                b = u % 2
                act.wait_ge(st, un * 6 + 6)
                act.wait_ge(pr, un * 2 + 1)
                act.activation(exp_a[:], score[:, b, :], ACT.Exp, bias=sm[:, u, 2:3]).then_inc(exps, 1)
                act.activation(exp_b[:], score[:, b, :], ACT.Exp, bias=sm[:, u, 3:4], scale=SLOPE).then_inc(exps, 1)

            with act.Fori(0, 2) as j:
                for g in range(2 * KT):
                    if g == EL_STEP + 1:
                        act.wait_ge(el_ps, j * 2 + 2)
                        for a in range(2):
                            act.activation(el_rows[:, a, :].rearrange("p (c q) -> p c q", q=P),
                                           pt_ps[:P, a * NT:(a + 1) * NT, :P], ACT.Copy).then_inc(el_free, 1)
                        exps_of(0, j * UPS)
                    if g in UNIT_STEPS:
                        u = UNIT_STEPS.index(g)
                        act.wait_ge(pt_done, j * UPS + (u + 1))
                        act.wait_ge(agg_done, j * UPS + (u + 1))
                        act.activation(pt_hi[:], pt_ps[:P, 0:NT, :P], ACT.Copy).then_inc(pt_hi_ready, 1)
                        if u + 1 < UPS:
                            exps_of(u + 1, j * UPS + (u + 1))
                    if g == KT - 1:
                        copy_k(j)
                    elif g == 2 * KT - 1:
                        for nt in range(NT):
                            act.wait_ge(proj_done, (j * 2 + (Z_CH + 1)) * NT + (nt + 1))
                            act.wait_ge(ones_v, 1)
                            act.wait_ge(kv_done, j * 2 + 1)
                            act.activation(v_sb[:, nt, :, 0:PAIR],
                                           ps[:P, nt, :].rearrange("p (r f) -> p r f", f=PAIR),
                                           ACT.Copy).then_inc(bank_free, 1)
                    ci = j * 2 + (Z_CH + g // KT)
                    step_split(ci, g % KT, ci * 2 + (g % KT // QUAD + 1))
                    if g == KT - 1:
                        exp_k(j)

            def hi_at(dst, pos):
                act.wait_ge(raw_in[pos % QUAD], 16 * (pos // QUAD + 1))
                act.activation(dst, w_raw[:, pos % QUAD, :], ACT.Copy).then_inc(w_hi_ready, 1)

            def hi_q(i):
                if i + QUAD < NU:
                    if i % 2 == 0:
                        act.wait_ge(w_used, (Z_CH + KV_CH) * (KT - 1) + i // 2 + 1)
                    else:
                        act.wait_ge(q_done, i + 1)
                    hi_at(w_hi[:, i % QUAD, :], stream_q(i + QUAD))

            def exp_q(r):
                for h, (_, kept) in enumerate(HALVES):
                    act.wait_ge(q_min, 2 * r + h + 1)
                    act.activation(q_t[:, r, kept], q_t[:, r, kept], ACT.Exp).then_inc(q_exp, 1)

            def attn_hi_part(t, b):
                act.wait_ge(attn_t, 2 * t + b + 1)
                act.activation(act_hi[:, 4 * b:4 * b + 4, t * P:(t + 1) * P],
                               ps[:, 4 + b, :].rearrange("p (c q) -> p c q", q=128)[:, :, :P],
                               ACT.Copy).then_inc(attn_hi, 1)

            act.wait_ge(agg_done, NUNIT + 1)
            act.wait_ge(kv_done, 2 * 2 + 1)
            for i in range(NU):
                hi_at(wo_hi[:, i % KT, i // KT * CH:(i // KT + 1) * CH], stream_o(i))
                hi_q(i)
                if i == NU - 1:
                    attn_hi_part(0, 0)
                if i % 2 == 1:
                    exp_q(i // 2)

            def second_ln(t):
                act.wait_ge(ln_b, LNB * t + 2)
                act.activation(ln[:, t, 1:2], ln[:, t, 0:1], ACT.Sqrt).then_inc(ln_std, 1)
                act.wait_ge(ln_b, LNB * t + 5)
                act.activation(centred[:, t, :], x_sb[:, t, :], ACT.Identity, bias=ln[:, t, 7:8]).then_inc(centred_in, 1)

            for t in range(NT):
                if t > 0:
                    attn_hi_part(t, 0)
                attn_hi_part(t, 1)
                if t >= 1:
                    second_ln(t - 1)
            second_ln(NT - 1)

            def round_rows(t, h):
                act.wait_ge(quant, 2 * t + h + 1)
                if t >= 2 and h == 0:
                    act.wait_ge(quant_ps, 2 * (t - 1))
                act.activation(quant_rows[:, t % 2, h * CH:(h + 1) * CH], rows[:, t % 2, h * CH:(h + 1) * CH],
                               ACT.Copy, bias=-MAGIC).then_inc(rounded, 1)

            def copy_quant_t(t, b):
                act.wait_ge(quant_ps, 2 * t + b + 1)
                if t >= 2:
                    act.wait_ge(ffn_done, 2 * (t - 1))
                act.activation(quant_t[:, t % 2, 4 * b:4 * b + 4, :P],
                               quant_bank(b).rearrange("p (c q) -> p c q", q=128)[:, :, :P],
                               ACT.Copy).then_inc(quant_ready, 1)

            act.wait_ge(ln_b, LNB * NT)
            act.activation(ident_bf[:], ident[:], ACT.Copy).then_inc(rounded, 1)
            for h in range(2):
                round_rows(0, h)
                copy_quant_t(0, h)
            for t in range(1, NT):
                for h in range(2):
                    round_rows(t, h)
                for b in range(2):
                    copy_quant_t(t, b)

        @block.vector
        def _(dve):
            def rstd_step(i, c, signal, n, stride=1):
                if i > 0:
                    dve.wait_ge(signal, n + stride * (i - 1) + 1)
                if i == 0:
                    dve.reciprocal(c[:, 2:3], c[:, 1:2]).then_inc(signal, 1)
                elif i == 1:
                    dve.scalar_tensor_tensor(c[:, 3:4], c[:, 2:3], c[:, 0:1], c[:, 2:3],
                                             ALU.mult, ALU.mult).then_inc(signal, 1)
                elif i == 2:
                    dve.tensor_scalar(c[:, 4:5], c[:, 3:4], -0.5, 1.5, ALU.mult, ALU.add).then_inc(signal, 1)
                else:
                    dve.tensor_tensor(c[:, 6:7], c[:, 4:5], c[:, 2:3], ALU.mult).then_inc(signal, 1)

            dve.wait_ge(edges_in, 16)
            dve.tensor_copy(dst_f[:], edge_i[:, 1, :]).then_inc(idx, 1)
            dve.tensor_scalar(half_i[:, 0, :], edge_i[:, 0, :], 1, None, ALU.arith_shift_right).then_inc(idx, 1)
            dve.tensor_scalar(half_i[:, 1, :], edge_i[:, 0, :], 1, None, ALU.bitwise_and).then_inc(idx, 1)
            dve.wait_ge(idx, 3)
            dve.tensor_copy(src_half[:], half_i[:, 0, :]).then_inc(idx, 1)
            dve.tensor_scalar(src_worth[:], half_i[:, 1, :], float(BASE - 1), 1.0, ALU.mult, ALU.add).then_inc(idx, 1)
            dve.wait_ge(idx, 5)
            dve.wait_ge(consts, 4)

            def onehots(n, s):
                dve.wait_ge(oh_used, n * SEG + (s + 1))
                dve.tensor_scalar(onehot_dst[:, s % RING, :], iota[:], dst_f[:, ds(n * SEG + s, 1)], None,
                                  ALU.is_equal).then_inc(oh_ready, 1)
                dve.tensor_scalar(onehot_src[:, s % RING, :], iota[:, :HALF], src_half[:, ds(n * SEG + s, 1)],
                                  src_worth[:, ds(n * SEG + s, 1)], ALU.is_equal, ALU.mult).then_inc(oh_ready, 1)

            def statistics(n, step):
                row = x_sb[:, ds(n, 1), :].rearrange("p a d -> p (a d)")
                c = ln[:, ds(n, 1), :].rearrange("p a d -> p (a d)")
                if step < 2:
                    if step == 0:
                        for a in ([n] if isinstance(n, int) else range(2, NT)):
                            dve.wait_ge(x_in[a], 16)
                    dve.bn_stats(bn[:, step, :], row[:, step * CH:(step + 1) * CH]).then_inc(ln_a, 1)
                elif step == 2:
                    dve.bn_aggr(mv[:], bn[:, :2, :].rearrange("p a b -> p (a b)")).then_inc(ln_a, 1)
                elif step == 3:
                    dve.wait_ge(ln_a, n * LNS + 3)
                    dve.tensor_scalar(c[:, 0:1], mv[:, 1:2], LN_EPS, None, ALU.add).then_inc(ln_a, 1)
                    dve.tensor_scalar(c[:, 7:8], mv[:, 0:1], -1.0, None, ALU.mult).then_inc(ln_a, 1)
                else:
                    if step == 4:
                        dve.wait_ge(ln_std, n + 1)
                    rstd_step(step - 4, c, ln_a, n * LNS + 5)

            def segment(n, rows_at):
                for s in range(SEG):
                    steps = [(t, s - first) for t, first in rows_at if 0 <= s - first < STATS]
                    for t, step in steps:
                        if step == 2:
                            dve.wait_ge(ln_a, t * LNS + 2)
                    onehots(n, s)
                    for t, step in steps:
                        statistics(t, step)

            segment(0, [(0, 0), (1, 8)])
            with dve.Fori(1, NT - 1) as n:
                segment(n, [(n + 1, 4)])
            segment(NT - 1, [])
            dve.wait_ge(f_abs, NU)
            dve.reduce_sum(abs_sum[:, NU:NU + 1], abs_sum[:, :NU], axis=AX.X).then_inc(fscale, 1)
            dve.wait_ge(row_t, 2 * NT)

            ups = 0
            dve.wait_ge(bank_free, NG * NT)
            for g in range(NG):
                pk, un, cs = packed[:, g, :, :], unpack[:], csum[:]
                dve.tensor_scalar(un, pk, -BASE / 2.0 + 48.0, 1.0 / BASE, ALU.add, ALU.mult).then_inc(up, 1)
                ups += 1
                dve.wait_ge(up, ups)
                dve.tensor_scalar(un, un, MAGIC, MAGIC, ALU.add, ALU.subtract).then_inc(up, 1)
                ups += 1
                dve.wait_ge(up, ups)
                dve.scalar_tensor_tensor(pk, un, -float(BASE), pk, ALU.mult, ALU.add).then_inc(up, 1)
                if g == 0:
                    dve.tensor_copy(cs, un).then_inc(up, 1)
                elif g < NG - 1:
                    dve.tensor_tensor(cs, cs, un, ALU.add).then_inc(up, 1)
                else:
                    dve.tensor_tensor(counts[:, :, 1:NPAD:2], cs[:, :, :NPAD // 2], un[:, :, :NPAD // 2],
                                      ALU.add).then_inc(up, 1)
                ups += 2
                dve.wait_ge(up, ups)
            for g in range(1, NG - 1):
                dve.tensor_tensor(packed[:, 0, :, :], packed[:, 0, :, :], packed[:, g, :, :], ALU.add).then_inc(up, 1)
                ups += 1
                dve.wait_ge(up, ups)
            dve.tensor_tensor(counts[:, :, 0:NPAD:2], packed[:, 0, :, :NPAD // 2],
                              packed[:, NG - 1, :, :NPAD // 2], ALU.add).then_inc(up, 1)
            ups += 1
            dve.wait_ge(up, ups)
            dve.tensor_scalar(no_edge[:], counts[:], 0.0, NEG, ALU.is_equal, ALU.mult).then_inc(up, 1)
            ups += 1
            dve.wait_ge(up, ups)
            dve.sem_inc(z_used, NT)

            dve.wait_ge(alr_in, 16)
            dve.sem_inc(el, 1)

            def take_z(c):
                for nt in range(NT):
                    for a in range(2):
                        for side in range(2):
                            if a == 0 and side == 0:
                                dve.wait_ge(bank_free, (c + NG) * NT + (nt + 1))
                                dve.wait_ge(el, (c * NT + nt) * ELS + 1)
                            col = side * HEADS + 2 * c + a
                            dve.scalar_tensor_tensor(
                                out=junk[:, 2 * a + side, :], in0=tmp[:, nt, a * F:(a + 1) * F], scalar=1.0,
                                in1=alr[:, side, c * CH + a * F:c * CH + (a + 1) * F], op0=ALU.mult, op1=ALU.mult,
                                accum_out=elr[:, nt, col:col + 1]).then_inc(el, 1)
                    dve.wait_ge(el, (c * NT + nt) * ELS + (ELS + 1))
                    dve.wait_ge(z_hi_ready, c * NT + (nt + 1))
                    dve.tensor_tensor(z_lo[:, nt, c * CH:(c + 1) * CH], tmp[:, nt, :],
                                      z_hi[:, nt, c * CH:(c + 1) * CH].bitcast(f32), ALU.subtract).then_inc(z_used, 1)

            def diagonals(j):
                for a in range(2):
                    if j > 0:
                        dve.wait_ge(el_ps, a + 1)
                    col = 2 * j + a
                    dve.tensor_tensor(diag[:, a, :, :],
                                      ident[:P, :P].rearrange("p (a q) -> p a q", a=1).broadcast_to([P, NT, P]),
                                      elr[:, :, col:col + 1].broadcast_to([P, NT, P]), ALU.mult).then_inc(diag_ready, 1)

            take_z(0)
            dve.wait_ge(fs_ps, 1)
            dve.tensor_scalar(scales[:, 0:1], ps[:, 7, 0:1], 1.0 / (D * D), None, ALU.mult).then_inc(fscale, 1)
            diagonals(0)
            dve.wait_ge(fscale, 2)
            dve.tensor_scalar(scales[:, 1:2], scales[:, 0:1], 0.5, None, ALU.mult).then_inc(fscale, 1)
            dve.tensor_scalar(scales[:, 2:3], scales[:, 0:1], -0.5, None, ALU.mult).then_inc(fscale, 1)
            dve.wait_ge(fscale, 4)
            take_z(1)
            dve.wait_ge(z_used, (1 + Z_CH) * NT)
            diagonals(1)

            dve.sem_inc(k_ready, NT)
            dve.memset(v_sb[:, :, :, PAIR:PAIR + 1], 1.0).then_inc(ones_v, 1)
            dve.sem_inc(pr, 1)

            def phi_min(j, nt):
                dve.wait_ge(bank_free, (j * 2 + (Z_CH + NG)) * NT + (nt + 1))
                dve.tensor_scalar(k_sb[:, nt, :], tmp[:, nt, :], 0.0, None, ALU.min).then_inc(k_min, 1)

            def phi_end(j, nt):
                dve.wait_ge(k_exp, j * NT + (nt + 1))
                dve.scalar_tensor_tensor(k_sb[:, nt, :], tmp[:, nt, :], 1.0, k_sb[:, nt, :],
                                         ALU.add, ALU.max).then_inc(k_ready, 1)

            def scores(u, j):
                a, dt = unit(u)
                un = j * UPS + u
                er = sm[:, u, 5:6]
                s0 = un * 6
                dve.tensor_scalar(er, elr[:, dt, ds(j * 2 + (HEADS + a), 1)], 0.0, None, ALU.add).then_inc(st, 1)
                dve.tensor_tensor_reduce(
                    out=score[:, u % 2, :], in0=no_edge[:, dt, :N],
                    in1=el_rows[:, a, :], scale=1.0, scalar=2 * NEG,
                    op0=ALU.add, op1=ALU.max, accum_out=sm[:, u, 0:1]).then_inc(st, 1)
                dve.wait_ge(st, s0 + 2)
                dve.tensor_scalar(sm[:, u, 1:2], sm[:, u, 0:1], er, NEG_FLOOR, ALU.add, ALU.max).then_inc(st, 1)
                dve.wait_ge(st, s0 + 3)
                dve.scalar_tensor_tensor(sm[:, u, 4:5], sm[:, u, 1:2], SLOPE, sm[:, u, 1:2],
                                         ALU.mult, ALU.max).then_inc(st, 1)
                dve.wait_ge(st, s0 + 4)
                dve.tensor_tensor(sm[:, u, 2:3], er, sm[:, u, 4:5], ALU.subtract).then_inc(st, 1)
                dve.scalar_tensor_tensor(sm[:, u, 3:4], er, SLOPE, sm[:, u, 4:5],
                                         ALU.mult, ALU.subtract).then_inc(st, 1)

            def probs(u, j):
                a, dt = unit(u)
                un = j * UPS + u
                dve.wait_ge(exps, un * 2 + 2)
                dve.tensor_tensor(exp_a[:], exp_a[:], exp_b[:], ALU.max).then_inc(pr, 1)
                dve.wait_ge(pr, un * 2 + 2)
                dve.tensor_tensor_reduce(out=prob[:, u % 2, :], in0=exp_a[:], in1=counts[:, dt, :N], scale=1.0,
                                         scalar=0.0, op0=ALU.mult, op1=ALU.add,
                                         accum_out=ssum[:, u:u + 1]).then_inc(pr, 1)

            def take(u, j):
                un = j * UPS + u
                dve.wait_ge(pt_hi_ready, un + 1)
                dve.tensor_tensor(pt_lo[:], pt_ps[:P, 0:NT, :P], pt_hi[:].bitcast(f32),
                                  ALU.subtract).then_inc(pt_ready, 1)

            def add_gat(u, j):
                a, dt = unit(u)
                un = j * UPS + u
                dve.tensor_scalar(rsum[:, u:u + 1], ssum[:, u:u + 1], 1e-30, None, ALU.max).then_inc(rs, 1)
                dve.wait_ge(rs, un * 2 + 1)
                dve.reciprocal(rsum[:, u:u + 1], rsum[:, u:u + 1]).then_inc(rs, 1)
                dve.wait_ge(rs, un * 2 + 2)
                dve.wait_ge(agg_done, un + 2)
                cols = ds(j * 2 * F + a * F, F)
                dve.scalar_tensor_tensor(x_sb[:, dt, cols], ps[:P, AGG, :F], rsum[:, u:u + 1],
                                         x_sb[:, dt, cols], ALU.mult, ALU.add).then_inc(agg_free, 1)

            with dve.Fori(0, 2) as j:
                dve.wait_ge(up, ups)
                dve.wait_ge(el_free, j * 2 + 2)
                scores(0, j)
                scores(1, j)
                probs(0, j)
                for u in range(UPS):
                    if u == PHI_UNIT:
                        for nt in range(NT):
                            phi_min(j, nt)
                    take(u, j)
                    if u + 2 < UPS:
                        scores(u + 2, j)
                    if u + 1 < UPS:
                        probs(u + 1, j)
                    if PHI_UNIT <= u < PHI_UNIT + NT:
                        phi_end(j, u - PHI_UNIT)
                    add_gat(u, j)
                for b in range(2):
                    dve.wait_ge(kv_done, j * 2 + (b + 2))
                    dve.wait_ge(kv_zero, 1)
                    for h in range(2):
                        rws = slice(h * DK, (h + 1) * DK)
                        src = ps[rws, 5 + b, :2 * (PAIR + 1)].rearrange("p (r f) -> p r f", f=PAIR + 1)
                        dst = kv_blocks[rws, ds(j * HP + 2 * b, 2), :]
                        dve.tensor_copy(dst[:, :, h * DK:(h + 1) * DK], src[:, :, h * DK:(h + 1) * DK]).then_inc(kv_free, 1)
                        dve.tensor_copy(dst[:, :, PAIR + h:PAIR + h + 1], src[:, :, PAIR:PAIR + 1]).then_inc(kv_free, 1)

            def ternary(u):
                b, c, k = u % 2, u // KT, u % KT
                dve.wait_ge(f_in[b], 16 * ((NU + u) // 2 + 1))
                if u >= 2:
                    dve.wait_ge(f_tern, u - 1)
                dve.tensor_scalar(above[:, b, :], f_raw[:, b, :], scales[:, 1:2], None, ALU.is_gt,
                                  saturate=False).then_inc(f_above, 1)
                dve.wait_ge(f_above, u + 1)
                dve.scalar_tensor_tensor(tern[:, k, c * CH:(c + 1) * CH], f_raw[:, b, :], scales[:, 2:3],
                                         above[:, b, :], ALU.is_lt, ALU.subtract,
                                         saturate=False).then_inc(f_tern, 1)

            def attention(t, parts):
                for b in parts:
                    dve.wait_ge(num_done, 3 * t + b + 1)
                    src, dv = num_of(b), den_of(t, b)
                    dve.tensor_scalar(dv, src[:, :, PAIR:PAIR + 2], DEN_EPS, None, ALU.add).then_inc(at_den, 1)
                for b in parts:
                    dve.wait_ge(at_den, 3 * t + b + 1)
                    dve.reciprocal(den_of(t, b), den_of(t, b)).then_inc(at_rec, 1)
                for b in parts:
                    dve.wait_ge(at_rec, 3 * t + b + 1)
                    if t >= 2 and b == 0:
                        dve.wait_ge(attn_t, 2 * (t - 1))
                    src, dv, n = num_of(b), den_of(t, b), PB[b]
                    dst = rows[:, t % 2, 3 * b * PAIR:(3 * b + n) * PAIR].rearrange("p (r f) -> p r f", f=PAIR)
                    for h in range(2):
                        dve.tensor_tensor(dst[:, :, h * DK:(h + 1) * DK], src[:, :, h * DK:(h + 1) * DK],
                                          dv[:, :, h:h + 1].broadcast_to([P, n, DK]), ALU.mult).then_inc(attn_ready, 1)

            def num_of(b):
                return ps[:P, 7 - b, :PB[b] * (PAIR + 2)].rearrange("p (r f) -> p r f", f=PAIR + 2)

            def den_of(t, b):
                return den[:, t % 2, 6 * b:6 * b + 2 * PB[b]].rearrange("p (r h) -> p r h", h=2)

            def attn_split(t, b):
                dve.wait_ge(attn_hi, 2 * t + b + 1)
                sl = (slice(None), slice(4 * b, 4 * b + 4), slice(t * P, (t + 1) * P))
                dve.tensor_tensor(act_lo[sl], ps[:, 4 + b, :].rearrange("p (c q) -> p c q", q=128)[:, :, :P],
                                  act_hi[sl].bitcast(f32), ALU.subtract).then_inc(attn_lo, 1)

            def q_ps(r, h):
                cols, kept = HALVES[h]
                return ps[:, 2 * (r % 2) + h, kept.start - cols.start:kept.stop - cols.start]

            for r in range(NPAIR):
                ternary(r)
                if r == NPAIR - 1:
                    attn_split(0, 0)
                if r == 4:
                    attention(0, [0])
                elif r == 6:
                    attention(0, [1])
                for h, (_, kept) in enumerate(HALVES):
                    dve.wait_ge(q_done, 2 * r + h + 1)
                    dve.tensor_scalar(q_t[:, r, kept], q_ps(r, h), 0.0, None,
                                      ALU.min).then_inc(q_min, 1)
                for h, (_, kept) in enumerate(HALVES):
                    dve.wait_ge(q_exp, 2 * r + h + 1)
                    dve.scalar_tensor_tensor(q_t[:, r, kept], q_ps(r, h), 1.0,
                                             q_t[:, r, kept], ALU.add, ALU.max).then_inc(q_ready, 1)

            def minimum(t, i):
                lo, hi = parts_of(t)[i]
                dve.tensor_reduce(extremes[:, t, 2 * i + 1:2 * i + 2], x_sb[:, t, lo:hi], axis=AX.X,
                                  op=ALU.min).then_inc(x1, 1)

            def second_ln(t):
                parts = parts_of(t)
                n, c = LNB * t, ln[:, t, :]
                piece = min(hi - lo for lo, hi in parts)
                for i, (lo, hi) in enumerate(parts):
                    p = 2 * t + i
                    dve.wait_ge(wo_done, p + 1)
                    dve.tensor_tensor_reduce(out=x_sb[:, t, lo:hi], in0=ps[:P, part_bank(t, i), :hi - lo],
                                             in1=x_sb[:, t, lo:hi], scale=1.0, scalar=-3.0e38,
                                             op0=ALU.add, op1=ALU.max,
                                             accum_out=extremes[:, t, 2 * i:2 * i + 1]).then_inc(x1, 1)
                    dve.wait_ge(x1, 3 * p + 1)
                    for at_ in range(lo, hi, piece):
                        last = dve.bn_stats(bn[:, at_ // piece, :], x_sb[:, t, at_:at_ + piece])
                        last.then_inc(x1 if at_ + piece == hi else ln_p, 1)
                    if i + 1 < len(parts):
                        minimum(t, i)
                np_ = len(parts)
                dve.wait_ge(x1, 3 * (2 * t + np_) - 1)
                if t == NT - 1:
                    dve.wait_ge(ln_p, 1)
                dve.bn_aggr(mv[:], bn[:, :D // piece, :].rearrange("p a b -> p (a b)")).then_inc(ln_b, 1)
                dve.wait_ge(ln_b, n + 1)
                dve.tensor_scalar(c[:, 0:1], mv[:, 1:2], LN_EPS, None, ALU.add).then_inc(ln_b, 1)
                dve.tensor_scalar(c[:, 7:8], mv[:, 0:1], -1.0, None, ALU.mult).then_inc(ln_b, 1)
                minimum(t, np_ - 1)
                dve.wait_ge(ln_b, n + 3)
                dve.wait_ge(ln_std, NT + t + 1)
                rstd_step(0, c, ln_b, n + 3, 2)
                dve.wait_ge(x1, 3 * (2 * t + np_))
                dve.tensor_scalar(extremes[:, t, :2 * np_], extremes[:, t, :2 * np_], c[:, 7:8], None,
                                  ALU.add).then_inc(ln_b, 1)
                rstd_step(1, c, ln_b, n + 3, 2)
                dve.wait_ge(ln_b, n + 5)
                dve.tensor_reduce(c[:, 8:9], extremes[:, t, :2 * np_], axis=AX.X, op=ALU.max,
                                  apply_absolute_value=True).then_inc(ln_b, 1)
                rstd_step(2, c, ln_b, n + 3, 2)
                dve.wait_ge(ln_b, n + 8)
                rstd_step(3, c, ln_b, n + 3, 2)
                dve.wait_ge(ln_b, n + 9)
                if t == 0:
                    dve.tensor_tensor(amax[:, 0:1], c[:, 8:9], c[:, 6:7], ALU.mult).then_inc(ln_b, 1)
                else:
                    dve.scalar_tensor_tensor(amax[:, t:t + 1], c[:, 8:9], c[:, 6:7], amax[:, t - 1:t],
                                             ALU.mult, ALU.max).then_inc(ln_b, 1)

            attention(0, [2])
            attn_split(0, 1)
            for t in range(NT):
                if t + 1 < NT:
                    attention(t + 1, range(3))
                    attn_split(t + 1, 0)
                    attn_split(t + 1, 1)
                    for u in (2 * t, 2 * t + 1):
                        ternary(NPAIR + u)
                second_ln(t)

            dve.wait_ge(gm_ps, 1)
            dve.reduce_max(scales[:P, 6:7], ps[:P, 4, :P], axis=AX.X).then_inc(gm, 1)
            dve.wait_ge(gm, 1)
            dve.tensor_scalar(scales[:P, 3:4], scales[:P, 6:7], 1.0 / 127.0, None, ALU.mult).then_inc(gm, 1)
            dve.wait_ge(gm, 2)
            dve.reciprocal(scales[:P, 4:5], scales[:P, 3:4]).then_inc(gm, 1)
            dve.wait_ge(gm, 3)
            dve.tensor_scalar(ln[:, :, 5], ln[:, :, 6], scales[:P, 4:5], None, ALU.mult).then_inc(gm, 1)
            dve.wait_ge(gm, 4)

            def quantise(t):
                for step, h in [(0, 0), (1, 0), (0, 1), (1, 1)] if t == 0 else [(0, 0), (0, 1), (1, 0), (1, 1)]:
                    half = slice(h * CH, (h + 1) * CH)
                    if step == 0:
                        dve.wait_ge(centred_in, t + 1)
                        dve.tensor_scalar(rows[:, t % 2, half], centred[:, t, half],
                                          ln[:, t, 5:6], 127.0, ALU.mult, ALU.min).then_inc(held, 1)
                    else:
                        dve.wait_ge(held, 2 * t + h + 1)
                        dve.tensor_scalar(rows[:, t % 2, half], rows[:, t % 2, half],
                                          -128.0, MAGIC, ALU.max, ALU.add).then_inc(quant, 1)

            def finish(t):
                dve.wait_ge(biased, t + 1)
                for i, (lo, hi) in enumerate(parts_of(t)):
                    dve.wait_ge(ffn_done, 2 * t + i + 1)
                    dve.scalar_tensor_tensor(x_sb[:, t, lo:hi], ps[:P, part_bank(t, i), :hi - lo],
                                             scales[:P, 5:6], x_sb[:, t, lo:hi],
                                             ALU.mult, ALU.add).then_inc(y_ready, 1)

            quantise(0)
            dve.scalar_tensor_tensor(scales[:P, 5:6], scales[:P, 3:4], -1.0, scales[:P, 0:1],
                                     ALU.mult, ALU.mult).then_inc(gm, 1)
            quantise(1)
            dve.wait_ge(gm, 5)
            for t in range(NT):
                if t + 2 < NT:
                    dve.wait_ge(rounded, 1 + 2 * (t + 1))
                    quantise(t + 2)
                finish(t)

        @block.tensor
        def _(pe):
            def three_pass(dst, a, b, first, last):
                pe.matmul(dst, a[0], b[0], start=first, stop=False)
                pe.matmul(dst, a[0], b[1], start=False, stop=False)
                return pe.matmul(dst, a[1], b[0], start=False, stop=last)

            def keep_clock(n):
                for _ in range(n):
                    pe.matmul(ps[:P, 5, :], zeros[:, :P], zeros[:], start=True, stop=True)

            def row_transposes(n):
                pe.wait_ge(row_ready, n + 1)
                for b in range(2):
                    if n > 0:
                        pe.wait_ge(row_t_in, 2 * (n - 1) + b + 1)
                    for c in range(4):
                        last = pe.transpose(pt_ps[:, 4 * b + c, :P],
                                            rows[:, n % 2, (4 * b + c) * 128:(4 * b + c + 1) * 128], ident[:P, :P])
                    last.then_inc(row_t, 1)

            def edge_tiles(q, opens=False):
                for s in range(RING):
                    pe.wait_ge(oh_ready, q * (2 * RING) + (2 * s + 2))
                    for nt in range(NT):
                        if opens and s == 0 and q > 0:
                            pe.wait_ge(bank_free, (g - 1) * NT + nt + 1)
                        last = pe.matmul(ps[:P, nt, :HALF], onehot_dst[:, s, nt * P:(nt + 1) * P],
                                         onehot_src[:, s, :], start=opens and s == 0, stop=False)
                    last.then_inc(oh_used, 1)

            pe.wait_ge(zeros_in, 1)
            keep_clock(6)
            pe.sem_inc(oh_used, RING)
            pe.wait_ge(consts, 4)
            for g, segs in enumerate(GROUP_SEGS):
                for n in segs:
                    if n > 0:
                        row_transposes(n - 1)
                    if n > segs[0]:
                        with pe.Fori(2 * n, 2 * n + 2) as q:
                            edge_tiles(q)
                    else:
                        edge_tiles(2 * n, opens=True)
                        if n == NT - 1:
                            row_transposes(n)
                        edge_tiles(2 * n + 1)
                for nt in range(NT):
                    pe.matmul(ps[:P, nt, :2], zeros[:, :P], zeros[:, :2], start=False, stop=True)\
                      .then_inc(count_done, 1)
            pe.wait_ge(act_ready, 2 * NT)

            def step(ci, k, unit_no, slot):
                pe.wait_ge(w_ready, unit_no)
                for nt in range(NT):
                    if k == 0:
                        pe.wait_ge(bank_free, (ci + NG - 1) * NT + (nt + 1))
                    rws = slice(nt * P, (nt + 1) * P)
                    last = three_pass(ps[:P, nt, :], (act_hi[:, k, rws], act_lo[:, k, rws]),
                                      (w_hi[:, slot, :], w_lo[:, slot, :]), k == 0, k == KT - 1)
                    if k == KT - 1:
                        last.then_inc(proj_done, 1)
                if k < KT - 1:
                    last.then_inc(w_used, 1)

            pe.wait_ge(fscale, 1)
            pe.matmul(ps[:, 7, 0:1], ones[:], abs_sum[:, NU:NU + 1], start=True, stop=True).then_inc(fs_ps, 1)

            with pe.Fori(0, Z_CH) as c:
                for k in range(KT):
                    step(c, k, c * KT + (k + 1), k % QUAD)

            pe.sem_inc(kv_done, 1)
            pe.sem_inc(agg_done, 1)
            pe.sem_inc(agg_free, 1)
            pe.sem_inc(kv_free, 1)
            with pe.Fori(0, 2) as j:
                for g in range(2 * KT):
                    u = UNIT_STEPS.index(g) if g in UNIT_STEPS else None
                    if u is not None:
                        a, dt = unit(u)
                        un = j * UPS + u
                        pe.wait_ge(pr, un * 2 + 3)
                        for s in range(NT):
                            last = pe.transpose(pt_ps[:P, s, :P], prob[:, u % 2, s * P:(s + 1) * P], ident[:P, :P])
                        last.then_inc(pt_done, 1)
                    ci = j * 2 + (Z_CH + g // KT)
                    step(ci, g % KT, ci * KT + (g % KT + 1), g % QUAD)
                    if g == EL_STEP:
                        for a in range(2):
                            pe.wait_ge(diag_ready, j * 2 + (a + 1))
                            if a == 0:
                                pe.wait_ge(kv_free, j * 8 + 1)
                            else:
                                pe.wait_ge(agg_free, j * UPS + 1)
                                pe.wait_ge(fscale, 2)
                            for s in range(NT):
                                last = pe.matmul(pt_ps[:P, a * NT + s, :P], ones[:P, :P], diag[:, a, s, :],
                                                 start=True, stop=True)
                            last.then_inc(el_ps, 1)
                    if u is not None:
                        pe.wait_ge(pt_ready, un + 1)
                        pe.wait_ge(agg_free, un + 1)
                        cols = ds(j * 2 * F + a * F, F)
                        for s in range(NT):
                            last = three_pass(ps[:P, AGG, :F], (pt_hi[:, s, :], pt_lo[:, s, :]),
                                              (z_hi[:, s, cols], z_lo[:, s, cols]), s == 0, s == NT - 1)
                        last.then_inc(agg_done, 1)
                pe.wait_ge(bank_free, (j * 2 + (Z_CH + 1 + NG)) * NT + NT)
                pe.wait_ge(k_ready, j * NT + 2 * NT)
                for b in range(2):
                    for r in range(2):
                        pr_ = 2 * b + r
                        for nt in range(NT):
                            last = pe.matmul(ps[:, 5 + b, r * (PAIR + 1):(r + 1) * (PAIR + 1)],
                                             k_sb[:, nt, pr_ * PAIR:(pr_ + 1) * PAIR], v_sb[:, nt, pr_, :],
                                             start=nt == 0, stop=nt == NT - 1)
                    last.then_inc(kv_done, 1)

            def numerator(t, b):
                if t > 0 and b < 2:
                    pe.wait_ge(attn_ready, 6 * t)
                elif t > 0:
                    pe.wait_ge(attn_lo, 2 * t)
                for r in range(3 * b, 3 * b + PB[b]):
                    if t == 0:
                        pe.wait_ge(q_ready, 2 * r + 1)
                    elif t == 1 and r == 0:
                        pe.wait_ge(q_ready, 2 * NPAIR)
                    i = r - 3 * b
                    last = pe.matmul(ps[:P, 7 - b, i * (PAIR + 2):(i + 1) * (PAIR + 2)],
                                     q_t[:, r, t * P:(t + 1) * P], kv_blocks[:, r, :], start=True, stop=True)
                last.then_inc(num_done, 1)

            def attn_transposes(t, b):
                pe.wait_ge(attn_ready, 6 * t + 4 + 2 * b)
                if t > 0:
                    pe.wait_ge(attn_lo, 2 * t - 1 + b)
                for c in range(4):
                    last = pe.transpose(ps[:, 4 + b, c * 128:c * 128 + P],
                                        rows[:, t % 2, (4 * b + c) * 128:(4 * b + c + 1) * 128], ident[:P, :P])
                last.then_inc(attn_t, 1)

            for i in range(NU):
                r, slot = i // 2, i % QUAD
                pe.wait_ge(w_ready, stream_q(i) + 1)
                for c in range(4):
                    k = 4 * (i % 2) + c
                    blk = slice(c * 128, (c + 1) * 128)
                    for h, (cols, _) in enumerate(HALVES):
                        if k == 0 and r >= 2:
                            pe.wait_ge(q_ready, 2 * (r - 2) + h + 1)
                        last = three_pass(ps[:, 2 * (r % 2) + h, :cols.stop - cols.start],
                                          (w_hi[:, slot, blk], w_lo[:, slot, blk]),
                                          (act_hi[:, k, cols], act_lo[:, k, cols]), k == 0, k == KT - 1)
                        if k == KT - 1:
                            last.then_inc(q_done, 1)
                if i % 2 == 0:
                    last.then_inc(w_used, 1)
                if i == 8:
                    pe.wait_ge(kv_free, 2 * 8 + 1)
                    pe.wait_ge(agg_free, NUNIT + 1)
                    numerator(0, 0)
                elif i == 12:
                    numerator(0, 1)
                elif i == 14:
                    attn_transposes(0, 0)

            def product(t, i, k0, k1):
                lo, hi = parts_of(t)[i]
                for k in range(k0, k1):
                    if t == 0:
                        pe.wait_ge(w_ready, stream_o(lo // CH * KT + k) + 1)
                    if k % 4 == 0:
                        pe.wait_ge(attn_lo, 2 * t + k // 4 + 1)
                    if k == 0:
                        if t < 2:
                            pe.wait_ge(q_ready, 2 * NPAIR - 2 + 2 * t)
                        else:
                            pe.wait_ge(x1, 3 * (2 * (t - 2) + i % 2) + 1 if i < 2 else 3 * 2 * (t - 1) + 1)
                    rws = slice(t * P, (t + 1) * P)
                    last = three_pass(ps[:P, part_bank(t, i), :hi - lo], (act_hi[:, k, rws], act_lo[:, k, rws]),
                                      (wo_hi[:, k, lo:hi], wo_lo[:, k, lo:hi]), k == 0, k == KT - 1)
                if k1 == KT:
                    last.then_inc(wo_done, 1)

            H, T2 = KT // 2, KT - 2
            product(0, 0, 0, 2)
            numerator(0, 2)
            product(0, 0, 2, H)
            product(0, 1, 0, 2)
            attn_transposes(0, 1)
            product(0, 1, 2, H)
            numerator(1, 0)
            numerator(1, 1)
            numerator(1, 2)
            product(0, 0, H, KT)
            product(0, 1, H, T2)
            attn_transposes(1, 0)
            attn_transposes(1, 1)
            product(0, 1, T2, KT)
            for t in range(1, NT):
                if t + 1 < NT:
                    for b in range(3):
                        numerator(t + 1, b)
                product(t, 0, 0, KT)
                product(t, 1, 0, H)
                if t + 1 < NT:
                    for b in range(2):
                        attn_transposes(t + 1, b)
                product(t, 1, H, KT)
            product(NT - 1, 2, 0, KT)

            keep_clock(14)
            pe.wait_ge(ln_b, LNB * NT)
            pe.matmul(ps[:P, 4, :P], amax[:, NT - 1:NT].broadcast_to([P, P]), ident[:P, :P],
                      start=True, stop=True).then_inc(gm_ps, 1)

            def quant_transposes(t, b):
                pe.wait_ge(rounded, 1 + 2 * t + b + 1)
                if t > 0:
                    pe.wait_ge(quant_ready, 2 * (t - 1) + b + 1)
                for c in range(4):
                    last = pe.transpose(quant_bank(b)[:, c * 128:c * 128 + P],
                                        quant_rows[:, t % 2, (4 * b + c) * 128:(4 * b + c + 1) * 128],
                                        ident_bf[:P, :P])
                last.then_inc(quant_ps, 1)

            def ffn(t, i, k0, k1):
                lo, hi = parts_of(t)[i]
                if t >= 2 and k0 == 0:
                    pe.wait_ge(y_ready, 2 * (t - 2) + i + 1)
                for k in range(k0, k1):
                    if k % H == 0:
                        pe.wait_ge(quant_ready, 2 * t + k // H + 1)
                    last = pe.matmul(ps[:P, part_bank(t, i), :hi - lo], quant_t[:, t % 2, k, :P],
                                     tern[:, k, lo:hi], start=k == 0, stop=k == KT - 1)
                if k1 == KT:
                    last.then_inc(ffn_done, 1)

            keep_clock(12)
            quant_transposes(0, 0)
            pe.wait_ge(f_tern, NU)
            ffn(0, 0, 0, H)
            quant_transposes(0, 1)
            ffn(0, 1, 0, H)
            ffn(0, 0, H, KT)
            for t in range(1, NT):
                for b in range(2):
                    quant_transposes(t, b)
                if t == 1:
                    ffn(0, 1, H, KT)
                else:
                    for i in range(1, len(PARTS)):
                        ffn(t - 1, i, 0, KT)
                ffn(t, 0, 0, KT)
            for i in range(1, len(LAST_PARTS)):
                ffn(NT - 1, i, 0, KT)


def _units(w):
    rows, cols = w.shape
    return w.reshape(rows // 128, 128, cols // 512, 512).transpose(2, 0, 1, 3).reshape(-1, 128, 512)


def _lay_out(src, dst, W, a_l, a_r, w_qkv, w_o, weight):
    import numpy as np

    heads, d, f = W.shape
    z = _units(W.transpose(1, 0, 2).reshape(d, heads * f))
    k, v = (_units(w_qkv[:, i * d:(i + 1) * d]) for i in (1, 2))
    q = w_qkv[:, :d].reshape(2, 4, 128, d // 128, 128).transpose(3, 0, 2, 1, 4).reshape(-1, 128, 512)
    o = _units(w_o)
    h = len(k) // 2
    first = 4
    mixed = [q[:first]]
    for i in range(len(o)):
        mixed.append(o[i:i + 1])
        if i + first < len(q):
            mixed.append(q[i + first:i + first + 1])
    weights = np.concatenate([z, k[:h], v[:h], k[h:], v[h:], *mixed])
    return {
        "edges": np.stack([src, dst]),
        "a_lr": np.stack([a_l.reshape(-1), a_r.reshape(-1)]),
        "weights": weights,
        "ffn_weights": _units(weight.T),
    }


def kernel(x, src, dst, L0_gnn_W, L0_gnn_a_l, L0_gnn_a_r, L0_mix_w_qkv, L0_mix_w_o, L0_ffn_weight, L0_ffn_bias):
    import numpy as np
    import concourse.bacc as bacc
    from concourse.bass_utils import run_bass_kernel_spmd

    arrays = {"x": np.asarray(x)}
    arrays.update(_lay_out(*(np.asarray(a) for a in (src, dst, L0_gnn_W, L0_gnn_a_l, L0_gnn_a_r,
                                                     L0_mix_w_qkv, L0_mix_w_o, L0_ffn_weight))))
    arrays["bias"] = np.asarray(L0_ffn_bias)
    nc = bacc.Bacc("TRN2", target_bir_lowering=False, num_devices=1)
    arrays = {f"in_{k}": np.ascontiguousarray(v) for k, v in arrays.items()}
    args = [nc.dram_tensor(k, v.shape, mybir.dt.from_np(v.dtype), kind="ExternalInput").ap()
            for k, v in arrays.items()]
    out = nc.dram_tensor("out_0", x.shape, mybir.dt.float32, kind="ExternalOutput").ap()
    gps_layer(nc, *args, out)
    result = run_bass_kernel_spmd(nc, [arrays], core_ids=[0])
    return result.results[0]["out_0"]
```
